# Optimizing a Trainium2 kernel written in Bass

```python
import numpy as np
import jax
import jax.numpy as jnp

def _softmax(x, axis=-1):
    return jax.nn.softmax(x, axis=axis)

def _gelu(x):
    return jax.nn.gelu(x, approximate=True)

def _silu(x):
    return jax.nn.silu(x)

def _sigmoid(x):
    return jax.nn.sigmoid(x)

def _layernorm(x, axis=-1, eps=1e-05):
    m = jnp.mean(x, axis=axis, keepdims=True)
    v = jnp.var(x, axis=axis, keepdims=True)
    return (x - m) / jnp.sqrt(v + eps)

def _scatter_add(tgt, idx, src, axis=0):
    return tgt.at[idx].add(src)

def _segment_sum(src, seg, n):
    return jax.ops.segment_sum(src, seg, n)
kernel_name = 'mk_seq_preln_d1_jaxref_r8_2d3d94'

def setup_inputs(seed: int=0):
    np.random.seed(seed)
    _w = jnp.asarray

    def _L0_attn_setup():
        import jax, jax.numpy as jnp
        import numpy as np
        N_HEADS = 16
        ROPE_BASE = 10000.0

        def _rope_tables(seq_len, d_head, dtype):
            inv_freq = 1.0 / ROPE_BASE ** (jnp.arange(0, d_head, 2, dtype=jnp.float32) / d_head)
            t = jnp.arange(seq_len, dtype=jnp.float32)
            freqs = t[:, None] * inv_freq[None, :]
            return (jnp.cos(freqs).astype(dtype), jnp.sin(freqs).astype(dtype))

        def _apply_rope(x, cos, sin):
            half = x.shape[-1] // 2
            x1, x2 = (x[..., :half], x[..., half:])
            return jnp.concatenate([x1 * cos - x2 * sin, x2 * cos + x1 * sin], axis=-1)
        key = jax.random.key(seed)
        k1, k2, k3 = jax.random.split(key, 3)
        d_model = 128
        x = jax.random.normal(k1, (2, 256, d_model), dtype=jnp.float32)
        w_qkv = jax.random.normal(k2, (d_model, 3 * d_model), dtype=jnp.float32) * d_model ** (-0.5)
        w_out = jax.random.normal(k3, (d_model, d_model), dtype=jnp.float32) * d_model ** (-0.5)
        return {'x': x, 'w_qkv': w_qkv, 'w_out': w_out}
    _L0_attn_in = _L0_attn_setup()

    def _L0_ffn_setup():
        import jax, jax.numpy as jnp
        import numpy as np
        B, S, D = (8, 512, 128)
        E, R, K = (6, 16, 2)
        key = jax.random.key(seed)
        ks = jax.random.split(key, 9)
        sc = 0.02
        return {'x': jax.random.normal(ks[0], (B, S, D), jnp.float32), 'base_W': jax.random.normal(ks[1], (D, D), jnp.float32) * sc, 'base_b': jax.random.normal(ks[2], (D,), jnp.float32) * sc, 'shared_A': jax.random.normal(ks[3], (R, D), jnp.float32) * sc, 'shared_B': jax.random.normal(ks[4], (D, R), jnp.float32) * sc, 'routed_A': jax.random.normal(ks[5], (E, R, D), jnp.float32) * sc, 'routed_B': jax.random.normal(ks[6], (E, D, R), jnp.float32) * sc, 'router_W': jax.random.normal(ks[7], (E, D), jnp.float32) * sc, 'router_b': jax.random.normal(ks[8], (E,), jnp.float32) * sc}
    _L0_ffn_in = _L0_ffn_setup()
    _d = {'L0_attn_x': _L0_attn_in['x'], 'L0_attn_w_qkv': _L0_attn_in['w_qkv'], 'L0_attn_w_out': _L0_attn_in['w_out'], 'L0_ffn_base_W': _L0_ffn_in['base_W'], 'L0_ffn_base_b': _L0_ffn_in['base_b'], 'L0_ffn_shared_A': _L0_ffn_in['shared_A'], 'L0_ffn_shared_B': _L0_ffn_in['shared_B'], 'L0_ffn_routed_A': _L0_ffn_in['routed_A'], 'L0_ffn_routed_B': _L0_ffn_in['routed_B'], 'L0_ffn_router_W': _L0_ffn_in['router_W'], 'L0_ffn_router_b': _L0_ffn_in['router_b']}
    _x0 = _d['L0_attn_x']
    _d['L0_attn_x'] = jax.random.normal(jax.random.fold_in(jax.random.key(seed), 1), (1, 2048, 128), dtype=_x0.dtype)
    del _x0
    return _d

def reference(L0_attn_x, L0_attn_w_qkv, L0_attn_w_out, L0_ffn_base_W, L0_ffn_base_b, L0_ffn_shared_A, L0_ffn_shared_B, L0_ffn_routed_A, L0_ffn_routed_B, L0_ffn_router_W, L0_ffn_router_b):

    def _L0_attn_ref(x, w_qkv, w_out):
        import jax, jax.numpy as jnp
        import numpy as np
        N_HEADS = 16
        ROPE_BASE = 10000.0

        def _rope_tables(seq_len, d_head, dtype):
            inv_freq = 1.0 / ROPE_BASE ** (jnp.arange(0, d_head, 2, dtype=jnp.float32) / d_head)
            t = jnp.arange(seq_len, dtype=jnp.float32)
            freqs = t[:, None] * inv_freq[None, :]
            return (jnp.cos(freqs).astype(dtype), jnp.sin(freqs).astype(dtype))

        def _apply_rope(x, cos, sin):
            half = x.shape[-1] // 2
            x1, x2 = (x[..., :half], x[..., half:])
            return jnp.concatenate([x1 * cos - x2 * sin, x2 * cos + x1 * sin], axis=-1)
        B, S, D = x.shape
        H = N_HEADS
        dh = D // H
        scale = dh ** (-0.5)
        qkv = x @ w_qkv
        q, k, v = jnp.split(qkv, 3, axis=-1)

        def to_heads(t):
            return t.reshape(B, S, H, dh).transpose(0, 2, 1, 3)
        q, k, v = (to_heads(q), to_heads(k), to_heads(v))
        cos, sin = _rope_tables(S, dh, x.dtype)
        q = _apply_rope(q, cos, sin)
        k = _apply_rope(k, cos, sin)
        scores = jnp.einsum('bhqd,bhkd->bhqk', q, k) * scale
        causal = jnp.tril(jnp.ones((S, S), dtype=bool))
        scores = jnp.where(causal, scores, jnp.finfo(scores.dtype).min)
        attn = jax.nn.softmax(scores, axis=-1)
        out = jnp.einsum('bhqk,bhkd->bhqd', attn, v)
        out = out.transpose(0, 2, 1, 3).reshape(B, S, D)
        return out @ w_out

    def _L0_ffn_ref(x, base_W, base_b, shared_A, shared_B, routed_A, routed_B, router_W, router_b):
        import jax, jax.numpy as jnp
        import numpy as np
        B, S, D = (8, 512, 128)
        E, R, K = (6, 16, 2)
        base_out = jax.lax.stop_gradient(jnp.einsum('bsi,oi->bso', x, base_W) + base_b)
        shared_out = jnp.einsum('bsr,or->bso', jnp.einsum('bsi,ri->bsr', x, shared_A), shared_B)
        logits = jnp.einsum('bsi,ei->bse', x, router_W) + router_b
        gate = jax.nn.softmax(logits, axis=-1)
        topk_w, topk_i = jax.lax.top_k(gate, K)
        sparse_w = jnp.sum(jax.nn.one_hot(topk_i, E, dtype=gate.dtype) * topk_w[..., None], axis=-2)
        sparse_w = sparse_w / (jnp.sum(sparse_w, axis=-1, keepdims=True) + 1e-06)
        h = jnp.einsum('bsi,eri->bser', x, routed_A)
        routed_outs = jnp.einsum('bser,eor->bseo', h, routed_B)
        routed_out = jnp.einsum('bseo,bse->bso', routed_outs, sparse_w)
        return base_out + shared_out + routed_out
    x = L0_attn_x
    x = x + _L0_attn_ref(_layernorm(x, axis=-1), L0_attn_w_qkv, L0_attn_w_out)
    x = x + _L0_ffn_ref(_layernorm(x, axis=-1), L0_ffn_base_W, L0_ffn_base_b, L0_ffn_shared_A, L0_ffn_shared_B, L0_ffn_routed_A, L0_ffn_routed_B, L0_ffn_router_W, L0_ffn_router_b)
    return x

_drawn_inputs = setup_inputs


def setup_inputs(seed=0):
    import zlib

    import numpy as np

    out = dict(_drawn_inputs(seed))
    spreads = {}
    factors = {'L0_ffn_base_b': 2.956,
     'L0_ffn_shared_A': 3.329,
     'L0_ffn_shared_B': 3.351,
     'L0_ffn_routed_A': 4.586,
     'L0_ffn_routed_B': 4.614,
     'L0_ffn_router_W': 5.675,
     'L0_ffn_router_b': 8.0}
    for name, (base, spread) in spreads.items():
        noise = np.random.default_rng([zlib.crc32(name.encode()), seed]).standard_normal(out[name].shape)
        drawn = base * np.exp(spread * noise) if base else spread * noise
        out[name] = jnp.asarray(drawn.astype(out[name].dtype))
    for name, factor in factors.items():
        out[name] = (out[name] * factor).astype(out[name].dtype)
    return out
```

```python
from contextlib import ExitStack

import concourse.bass as bass
import numpy as np
from concourse import mybir

F32 = mybir.dt.float32
BF16 = mybir.dt.bfloat16
I32 = mybir.dt.int32
ALU = mybir.AluOpType
ACT = mybir.ActivationFunctionType
AX = mybir.AxisListType

P = 128
S = 2048
D = 128
H = 16
DH = D // H
NP = H // 2
CH = 512
NC = S // CH
TC = CH // P
NT = S // P
GH = 4
NG = H // GH
E, R = 6, 16
RD = R + E * R
SCALE = DH ** -0.5
EPS = 1e-5
BOUND = 60.0
MASKED = -3.0e38

HALF = P // 2
SHIFT_ROWS = 3
SLOTS = ((0, 0), (0, 1), (1, 0), (1, 1), (0, 2), (2, 0))

NS = 3
NPB = 7
LAG = 5


def plan():
    units, blocks = [], []
    for c in range(NC):
        for g in range(NG):
            work = [("full", kt) for kt in range(4 * c + 1)] + [("ends", 4 * c + 1), ("mid", 4 * c + 2)]
            for n, (kind, kt) in enumerate(work):
                diagonal = kt >= 4 * c
                mine = []
                for pair in ((0, 1),) if kind == "mid" else ((0,), (1,)):
                    mine.append(len(units))
                    units.append(dict(c=c, g=g, kind=kind, kt=kt, pairs=pair, diagonal=diagonal, block=len(blocks)))
                blocks.append(dict(c=c, g=g, kind=kind, kt=kt, units=mine, first=n == 0,
                                   last=n == len(work) - 1, diagonal=diagonal))
    return units, blocks


UNITS, BLOCKS = plan()
MASKS_THROUGH = [sum(u["diagonal"] for u in UNITS[:n + 1]) for n in range(len(UNITS))]
FIRST_UNIT = [next(n for n, u in enumerate(UNITS) if u["c"] == c) for c in range(NC)]


def pieces(unit_kind):
    return {"full": [(0, 0, CH, 0)],
            "ends": [(0, P, CH - P, 0), (2, CH - P, P, CH - P)],
            "mid": [(0, 2 * P, 2 * P, 0)]}[unit_kind]


PROJECT = ("T", "Q", "QS", "K", "KS", "V", "B")
FINISH = ("N0", "N1", "N2", "N3", "A", "O", "X", "R", "W", "U", "F")


def schedule():
    jobs = [(name, 0) for name in PROJECT]
    at = {}
    for c in range(NC):
        begin = FIRST_UNIT[c]
        end = FIRST_UNIT[c + 1] if c + 1 < NC else len(UNITS)
        todo = [(name, c + 1) for name in PROJECT] if c + 1 < NC else []
        todo += [(name, c - 1) for name in FINISH] if c else []
        lead = LAG + 3 if c else 1
        room = (end - begin - lead - 6) / max(1, len(todo))
        for n, job in enumerate(todo):
            at.setdefault(begin + lead + int(n * room), []).append(len(jobs))
            jobs.append(job)
    tail = list(range(len(jobs), len(jobs) + len(FINISH)))
    jobs += [(name, NC - 1) for name in FINISH]
    return jobs, at, tail


JOBS, JOBS_AT, TAIL_JOBS = schedule()
JOB = {job: n for n, job in enumerate(JOBS)}
PRODUCTS = [sum(name != "W" for name, _ in JOBS[:n + 1]) for n in range(len(JOBS))]


def build(nc, x, w_qkv, rope_c, rope_s, w_out, w_down, w_up, w_base, router_b, ident, head_sum,
          lower, future, out):
    x_t = x.rearrange("(n p) d -> p n d", p=P)
    out_t = out.rearrange("(n p) d -> p n d", p=P)
    with ExitStack() as ctx:
        def sb(name, shape, dt=F32):
            return ctx.enter_context(nc.sbuf_tensor(name, shape, dt))

        def sem(name):
            return ctx.enter_context(nc.semaphore(name))

        wqkv = sb("wqkv", [P, 5, D])
        wout = sb("wout", [P, D])
        wdown = sb("wdown", [P, RD + E])
        wup = sb("wup", [RD + 1, D])
        wbase = sb("wbase", [P, D])
        rbias = sb("rbias", [P, E])
        idf = sb("idf", [P, P])
        idb = sb("idb", [P, P], BF16)
        hsum = sb("hsum", [P, H])
        low = sb("low", [P, E, E])
        fut = sb("fut", [P, P])
        futb = sb("futb", [P, P], BF16)
        cosT = sb("cosT", [P, 2, CH])
        sinT = sb("sinT", [P, 2, CH])
        xs = sb("xs", [P, NT, D])
        kst = sb("kst", [P, H, S], BF16)
        qst = sb("qst", [P, NP, S], BF16)
        va = sb("va", [P, NT, H, DH + 1])
        pbuf = sb("pbuf", [P, NPB, 2 * CH])
        oT = sb("oT", [P, 2, NG, CH])
        xn = sb("xn", [P, TC, D])
        xnT = sb("xnT", [P, CH])
        rot = sb("rot", [P, 2, CH])
        rest = sb("rest", [P, 2, CH])
        parts = sb("parts", [P, 3, 2, CH], BF16)
        stats = sb("stats", [P, TC, 6])
        mv = sb("mv", [P, TC, 2])
        var = sb("var", [P, TC])
        rstd = sb("rstd", [P, TC])
        sq = sb("sq", [P, TC])
        absmax = sb("absmax", [P, 2])
        kmax = sb("kmax", [P, 1])
        bnd = sb("bnd", [P, 1])
        bmax = sb("bmax", [1, 1])
        flag = sb("flag", [1, NC], I32)
        rec = sb("rec", [P, H])
        att = sb("att", [P, TC, D])
        x1 = sb("x1", [P, TC, D])
        low_rank = sb("low_rank", [P, TC, P])
        lg = sb("lg", [P, TC, E])
        small = sb("small", [P, TC])
        gate = sb("gate", [P, TC, E])
        above = sb("above", [P, TC, E, E])
        ties = sb("ties", [P, TC, E, E])
        rank = sb("rank", [P, TC, E])
        rmax = sb("rmax", [P, TC, H])
        mparts = sb("mparts", [P, TC, 2, SHIFT_ROWS, NP])
        mrest = sb("mrest", [P, TC, H])
        mbf = sb("mbf", [P, TC, H], BF16)
        mrow = sb("mrow", [2 * SHIFT_ROWS * NP, CH], BF16)

        ps = ctx.enter_context(nc.psum_tensor("ps", [P, NS, 2, CH], F32))
        po = ctx.enter_context(nc.psum_tensor("po", [P, CH], F32))
        pm = ctx.enter_context(nc.psum_tensor("pm", [P, CH], F32))
        pm_t = pm[:, :].rearrange("p (t d) -> p t d", t=TC)

        x_in = [sem(f"x_in{c}") for c in range(NC)]
        rope_in = [sem(f"rope_in{c}") for c in range(NC)]
        qkv_in, const_in, ffn_in = sem("qkv_in"), sem("const_in"), sem("ffn_in")
        zeroed = sem("zeroed")
        ones_set = sem("ones_set")
        vec = sem("vec")
        parts_ready = sem("parts_ready")
        stacked = [sem(f"stacked{c}") for c in range(NC)]
        v_ready = sem("v_ready")
        flag_ready = sem("flag_ready")
        job_fed = sem("job_fed")
        job_full = sem("job_full")
        scores_ready = sem("scores_ready")
        exp_ready = sem("exp_ready")
        masked = sem("masked")
        block_done = sem("block_done")
        o_free = sem("o_free")
        logits_ready = sem("logits_ready")
        logits_exp = sem("logits_exp")
        y_ready = sem("y_ready")
        stored = sem("stored")
        max_scores = [sem(f"max_scores{c}") for c in range(NC)]
        max_taken = [sem(f"max_taken{c}") for c in range(NC)]
        max_vec = [sem(f"max_vec{c}") for c in range(NC)]
        max_rows = [sem(f"max_rows{c}") for c in range(NC)]
        max_stacked = [sem(f"max_stacked{c}") for c in range(NC)]

        ybuf = sb("ybuf", [P, TC, D])
        block = ctx.enter_context(nc.Block())

        def at_flag(engine, c):
            engine.wait_ge(flag_ready, c + 1)
            return engine.value_load(flag[0:1, c:c + 1], min_val=0, max_val=1)

        @block.sync
        def _(sp):
            def load_chunk(c):
                cols = slice(c * CH, (c + 1) * CH)
                sp.dma_start(xs[:, c * TC:(c + 1) * TC, :], x_t[:, c * TC:(c + 1) * TC, :]).then_inc(x_in[c], 16)
                if c == 0:
                    sp.dma_start(idf[:, :], ident).then_inc(const_in, 16)
                    sp.dma_start(wqkv[:, :, :], w_qkv).then_inc(qkv_in, 16)
                sp.dma_start(cosT[:, c % 2, :], rope_c[:, cols]).then_inc(rope_in[c], 16)
                sp.dma_start(sinT[:, c % 2, :], rope_s[:, cols]).then_inc(rope_in[c], 16)

            def stack_parts(c):
                sp.wait_ge(parts_ready, c + 1)
                sp.wait_ge(zeroed, c + 1)
                cols = slice(c * CH, (c + 1) * CH)
                for r, (k_part, q_part) in enumerate(SLOTS):
                    for e in range(2):
                        row = e * HALF + DH * (r + 1)
                        src = slice(e * HALF, (e + 1) * HALF)
                        sp.dma_start(kst[row:row + DH, e::2, cols], parts[src, k_part, 1, :]).then_inc(stacked[c], 16)
                        sp.dma_start(qst[row:row + DH, :, cols], parts[src, q_part, 0, :]).then_inc(stacked[c], 16)

            def stack_maxima(c):
                with sp.If(at_flag(sp, c) > 0):
                    sp.wait_ge(max_rows[c], 1)
                    n = SHIFT_ROWS * NP
                    for e in range(2):
                        sp.dma_start(qst[e * HALF:e * HALF + SHIFT_ROWS, :, c * CH:(c + 1) * CH],
                                     mrow[e * n:(e + 1) * n, :]).then_inc(max_stacked[c], 16)
                    sp.wait_ge(max_stacked[c], 32)

            def store(c):
                sp.wait_ge(y_ready, c + 1)
                sp.dma_start(out_t[:, c * TC:(c + 1) * TC, :], ybuf[:, :, :]).then_inc(stored, 16)

            load_chunk(0)
            sp.dma_start(hsum[:, :], head_sum).then_inc(const_in, 16)
            sp.dma_start(fut[:, :], future).then_inc(const_in, 16)
            sp.dma_start(low[:, :, :], lower).then_inc(const_in, 16)
            stack_parts(0)
            load_chunk(1)
            for dst, src in ((wout, w_out), (wdown, w_down), (wup, w_up), (wbase, w_base), (rbias, router_b)):
                sp.dma_start(dst[:, :], src).then_inc(ffn_in, 16)
            stack_maxima(0)
            for c in range(1, NC):
                stack_parts(c)
                if c + 1 < NC:
                    load_chunk(c + 1)
                if c >= 2:
                    store(c - 2)
                stack_maxima(c)
            store(NC - 2)
            store(NC - 1)
            sp.wait_ge(stored, 16 * NC)

        @block.gpsimd
        def _(pool):
            for c in range(NC):
                cols = slice(c * CH, (c + 1) * CH)
                nc.gpsimd.memset(qst[:, :, cols], 0.0)
                nc.gpsimd.memset(kst[:, :, cols], 0.0).then_inc(zeroed, 1)
                if c == 0:
                    clear_rows = [None]
            for u, unit in enumerate(UNITS):
                if not unit["diagonal"]:
                    continue
                pool.wait_ge(exp_ready, u + 1)
                buf = pbuf[:, u % NPB, :]
                if unit["kind"] == "mid":
                    edges = [buf.rearrange("p (h q) -> p h q", h=4)[:, :, 0:P]]
                else:
                    heads = buf.rearrange("p (h q) -> p h q", h=2)
                    edges = [heads[:, :, place:place + P] for _, _, _, place in pieces(unit["kind"])]
                for edge in edges:
                    ins = nc.gpsimd.affine_select(out=edge, in_=edge, compare_op=ALU.is_ge, fill=0.0, base=0,
                                                  pattern=[[0, edge.shape[1]], [1, P]], channel_multiplier=-1)
                ins.then_inc(masked, 1)

        @block.scalar
        def _(act):
            for u, unit in enumerate(UNITS):
                act.wait_ge(scores_ready, u + 1)
                if u >= NPB:
                    act.wait_ge(block_done, UNITS[u - NPB]["block"] + 1)
                nc.scalar.activation(pbuf[:, u % NPB, :], ps[:, u % NS, :, :].rearrange("p b q -> p (b q)"),
                                     ACT.Exp, scale=SCALE).then_inc(exp_ready, 1)
                for n in JOBS_AT.get(u, ()):
                    if JOBS[n][0] == "R":
                        act.wait_ge(logits_ready, JOBS[n][1] + 1)
                        nc.scalar.activation(gate[:, :, :], lg[:, :, :], ACT.Exp).then_inc(logits_exp, 1)
            act.wait_ge(logits_ready, NC)
            nc.scalar.activation(gate[:, :, :], lg[:, :, :], ACT.Exp).then_inc(logits_exp, 1)

        @block.vector
        def _(dve):
            steps = [0]

            def then(ins):
                steps[0] += 1
                ins.then_inc(vec, 1)
                dve.wait_ge(vec, steps[0])

            def inverse_sqrt():
                then(nc.vector.tensor_scalar(var[:, :], mv[:, :, 1], EPS, None, ALU.add))
                then(nc.vector.tensor_scalar(rstd[:, :].bitcast(I32), var[:, :].bitcast(I32), -0.5, float(0x5F3759DF),
                                             ALU.mult, ALU.add))
                for _ in range(4):
                    then(nc.vector.tensor_tensor(sq[:, :], rstd[:, :], rstd[:, :], ALU.mult))
                    then(nc.vector.scalar_tensor_tensor(sq[:, :], sq[:, :], -0.5, var[:, :], ALU.mult, ALU.mult))
                    then(nc.vector.scalar_tensor_tensor(rstd[:, :], sq[:, :], 1.5, rstd[:, :], ALU.add, ALU.mult))

            def layernorm(src):
                for t in range(TC):
                    ins = nc.vector.bn_stats(stats[:, t, :], src(t))
                then(ins)
                for t in range(TC):
                    ins = nc.vector.bn_aggr(mv[:, t, :], stats[:, t, :])
                then(ins)
                inverse_sqrt()
                for t in range(TC):
                    ins = nc.vector.tensor_scalar(xn[:, t, :], src(t), mv[:, t, 0:1], rstd[:, t:t + 1],
                                                  ALU.subtract, ALU.mult)
                then(ins)

            def evacuate(block_index):
                b = BLOCKS[block_index]
                dve.wait_ge(block_done, block_index + 1)
                nc.vector.tensor_copy(oT[:, b["c"] % 2, b["g"], :], po[:, :]).then_inc(o_free, 1)

            def rotate(which, c, swapped):
                if not swapped:
                    dve.wait_ge(rope_in[c], 32)
                    then(nc.vector.tensor_tensor(rot[:, which, :], pm[:, :], cosT[:, c % 2, :], ALU.mult))
                else:
                    then(nc.vector.tensor_tensor(rest[:, which, :], pm[:, :], sinT[:, c % 2, :], ALU.mult))
                    then(nc.vector.tensor_tensor(rot[:, which, :], rot[:, which, :], rest[:, which, :], ALU.add))

            def split(c):
                if c:
                    dve.wait_ge(stacked[c - 1], 16 * 4 * len(SLOTS))
                then(nc.vector.tensor_copy(parts[:, 0, :, :], rot[:, :, :]))
                then(nc.vector.tensor_tensor(rest[:, :, :], rot[:, :, :], parts[:, 0, :, :], ALU.subtract))
                then(nc.vector.tensor_copy(parts[:, 1, :, :], rest[:, :, :]))
                nc.vector.tensor_tensor(parts[:, 2, :, :], rest[:, :, :], parts[:, 1, :, :],
                                        ALU.subtract).then_inc(parts_ready, 1)

            def bound(c):
                then(nc.vector.tensor_reduce(absmax[:, :], rot[:, :, :], AX.X, ALU.max, apply_absolute_value=True))
                if c:
                    then(nc.vector.tensor_tensor(kmax[:, :], kmax[:, :], absmax[:, 1:2], ALU.max))
                else:
                    then(nc.vector.tensor_copy(kmax[:, :], absmax[:, 1:2]))
                then(nc.vector.tensor_tensor(bnd[:, :], absmax[:, 0:1], kmax[:, :], ALU.mult))

            def choose():
                shape = [P, TC, E, E]
                this, other = (gate[:, :, :].unsqueeze(3).broadcast_to(shape), gate[:, :, :].unsqueeze(2).broadcast_to(shape))
                per_token = small[:, :].unsqueeze(2).broadcast_to([P, TC, E])
                then(nc.vector.tensor_reduce(small[:, :], gate[:, :, :], AX.X, ALU.add))
                then(nc.vector.reciprocal(small[:, :], small[:, :]))
                then(nc.vector.tensor_tensor(gate[:, :, :], gate[:, :, :], per_token, ALU.mult))
                nc.vector.tensor_tensor(above[:, :, :, :], other, this, ALU.is_gt)
                then(nc.vector.tensor_tensor(ties[:, :, :, :], other, this, ALU.is_equal))
                then(nc.vector.tensor_tensor(ties[:, :, :, :], ties[:, :, :, :],
                                             low[:, :, :].unsqueeze(1).broadcast_to(shape), ALU.mult))
                then(nc.vector.tensor_tensor(above[:, :, :, :], above[:, :, :, :], ties[:, :, :, :], ALU.add))
                then(nc.vector.tensor_reduce(rank[:, :, :], above[:, :, :, :], AX.X, ALU.add))
                then(nc.vector.scalar_tensor_tensor(gate[:, :, :], rank[:, :, :], 1.5, gate[:, :, :], ALU.is_lt, ALU.mult))
                then(nc.vector.tensor_reduce(small[:, :], gate[:, :, :], AX.X, ALU.add))
                then(nc.vector.tensor_scalar(small[:, :], small[:, :], 1e-6, None, ALU.add))
                then(nc.vector.reciprocal(small[:, :], small[:, :]))
                then(nc.vector.tensor_tensor(gate[:, :, :], gate[:, :, :], per_token, ALU.mult))

            def take(n):
                name, c = JOBS[n]
                if name != "W":
                    dve.wait_ge(job_full, PRODUCTS[n])
                tiles = slice(c * TC, (c + 1) * TC)
                if name in ("T", "A", "X"):
                    then(nc.vector.tensor_copy(xnT[:, :], pm[:, :]))
                elif name in ("Q", "QS"):
                    rotate(0, c, name == "QS")
                elif name in ("K", "KS"):
                    rotate(1, c, name == "KS")
                    if name == "KS":
                        split(c)
                        bound(c)
                elif name == "V":
                    nc.vector.tensor_copy(va[:, tiles, :, 0:DH],
                                          pm[:, :].rearrange("p (t h d) -> p t h d", t=TC, h=H)).then_inc(v_ready, 1)
                    dve.wait_ge(v_ready, c + 1)
                elif name == "B":
                    then(nc.vector.tensor_reduce(bmax[:, :], pm[0:1, 0:H], AX.X, ALU.max))
                    nc.vector.tensor_scalar(flag[0:1, c:c + 1], bmax[:, :], BOUND / SCALE, None,
                                            ALU.is_gt).then_inc(flag_ready, 1)
                elif name[0] == "N":
                    t = int(name[1])
                    heads = pm[:, :].rearrange("p (h d) -> p h d", h=H)
                    then(nc.vector.reciprocal(rec[:, :], heads[:, :, DH]))
                    then(nc.vector.tensor_tensor(att[:, t, :].rearrange("p (h d) -> p h d", h=H), heads[:, :, 0:DH],
                                                 rec[:, :].unsqueeze(2).broadcast_to([P, H, DH]), ALU.mult))
                elif name == "O":
                    then(nc.vector.tensor_tensor(x1[:, :, :], pm_t, xs[:, tiles, :], ALU.add))
                    layernorm(lambda t: x1[:, t, :])
                elif name == "R":
                    dve.wait_ge(ffn_in, 16 * 5)
                    nc.vector.tensor_copy(low_rank[:, :, 0:RD], pm_t[:, :, 0:RD])
                    then(nc.vector.tensor_tensor(lg[:, :, :], pm_t[:, :, RD:RD + E],
                                                 rbias[:, :].unsqueeze(1).broadcast_to([P, TC, E]), ALU.add))
                    then(nc.vector.tensor_reduce(small[:, :], lg[:, :, :], AX.X, ALU.max))
                    nc.vector.tensor_tensor(lg[:, :, :], lg[:, :, :], small[:, :].unsqueeze(2).broadcast_to([P, TC, E]),
                                            ALU.subtract).then_inc(logits_ready, 1)
                elif name == "W":
                    dve.wait_ge(logits_exp, c + 1)
                    choose()
                    routed = low_rank[:, :, R:RD].rearrange("p t (e r) -> p t e r", e=E)
                    then(nc.vector.tensor_tensor(routed, routed,
                                                 gate[:, :, :].unsqueeze(3).broadcast_to([P, TC, E, R]), ALU.mult))
                elif name == "U":
                    then(nc.vector.tensor_copy(att[0:RD + 1, :, :].rearrange("p t d -> p (t d)"), pm[0:RD + 1, :]))
                elif name == "F":
                    if c:
                        dve.wait_ge(stored, 16 * c)
                    nc.vector.tensor_tensor(ybuf[:, :, :], pm_t, x1[:, :, :], ALU.add).then_inc(y_ready, 1)
                    dve.wait_ge(y_ready, c + 1)
                if n + 1 < len(JOBS) and JOBS[n + 1][0] == "T":
                    normalise(JOBS[n + 1][1])
                if n + 1 < len(JOBS) and JOBS[n + 1][0] != "W":
                    nc.vector.engine_nop().then_inc(job_fed, 1)

            def normalise(c):
                dve.wait_ge(x_in[c], 16)
                layernorm(lambda t: xs[:, c * TC + t, :])

            def row_maxima(c):
                with dve.If(at_flag(dve, c) > 0):
                    for t in range(TC):
                        width = (c * TC + t + 1) * P
                        with dve.Fori(0, NP) as pair:
                            for e in range(2):
                                dve.wait_ge(max_scores[c], t * H + pair * 2 + (e + 1))
                                nc.vector.tensor_reduce(
                                    rmax[:, t, bass.ds(pair * 2 + e, 1)],
                                    ps[:, :, :, :].rearrange("p a b q -> p (a b q)")[:, 0:width],
                                    AX.X, ALU.max).then_inc(max_taken[c], 1)
                    dve.wait_ge(max_taken[c], TC * H)
                    n = [0]

                    def after(ins):
                        n[0] += 1
                        ins.then_inc(max_vec[c], 1)
                        dve.wait_ge(max_vec[c], n[0])
                    after(nc.vector.tensor_scalar(mrest[:, :, :], rmax[:, :, :], -1.0, None, ALU.mult))
                    by_half = mbf[:, :, :].rearrange("p t (n e) -> p t e n", e=2)
                    for part in range(SHIFT_ROWS):
                        after(nc.vector.tensor_copy(mbf[:, :, :], mrest[:, :, :]))
                        for t in range(TC):
                            after(nc.vector.tensor_copy(mparts[:, t, :, part, :], by_half[:, t, :, :]))
                        if part + 1 < SHIFT_ROWS:
                            after(nc.vector.tensor_tensor(mrest[:, :, :], mrest[:, :, :], mbf[:, :, :], ALU.subtract))
                    dve.wait_ge(max_scores[c], TC * H + 1)
                    nc.vector.tensor_copy(mrow[:, :], ps[0:2 * SHIFT_ROWS * NP, 0, 0, :]).then_inc(max_rows[c], 1)
                    dve.wait_ge(max_rows[c], 1)
                nc.vector.engine_nop()

            nc.vector.memset(po[:, :], 0.0).then_inc(ones_set, 1)
            nc.vector.memset(va[:, :, :, DH:DH + 1], 1.0).then_inc(ones_set, 1)
            nc.vector.memset(low_rank[:, :, RD:P], 1.0).then_inc(ones_set, 1)
            normalise(0)
            nc.vector.engine_nop().then_inc(job_fed, 1)
            for n in range(len(PROJECT)):
                take(n)
                if n == 1:
                    dve.wait_ge(zeroed, NC)
                    for e in range(2):
                        nc.vector.memset(kst[e * HALF:e * HALF + SHIFT_ROWS, e::2, :], 1.0).then_inc(ones_set, 1)
                    dve.wait_ge(const_in, 16 * 4)
                    nc.vector.tensor_copy(idb[:, :], idf[:, :]).then_inc(ones_set, 1)
                    nc.vector.tensor_copy(futb[:, :], fut[:, :]).then_inc(ones_set, 1)
            row_maxima(0)
            ends = {b["units"][-1] + LAG: n for n, b in enumerate(BLOCKS) if b["last"]}
            for u in range(len(UNITS)):
                if u in FIRST_UNIT[1:]:
                    row_maxima(FIRST_UNIT.index(u))
                if u in ends:
                    evacuate(ends[u])
                for n in JOBS_AT.get(u, ()):
                    take(n)
            evacuate(len(BLOCKS) - 1)
            for n in TAIL_JOBS:
                take(n)

        @block.tensor
        def _(pe):
            def scores(u):
                unit = UNITS[u]
                c, g, kt = unit["c"], unit["g"], unit["kt"]
                if u >= NS:
                    pe.wait_ge(exp_ready, u - NS + 1)
                per_pair = len(unit["pairs"])
                for at, pair in enumerate(unit["pairs"]):
                    for e in range(2):
                        head = g * GH + pair * 2 + e
                        for dk, q0, n, place in pieces(unit["kind"]):
                            bank = e if per_pair == 1 else at
                            place += 0 if per_pair == 1 else e * 2 * P
                            key = (kt + dk) * P
                            q = c * CH + q0
                            ins = nc.tensor.matmul(ps[:, u % NS, bank, place:place + n], kst[:, head, key:key + P],
                                                   qst[:, g * 2 + pair, q:q + n], start=True, stop=True)
                ins.then_inc(scores_ready, 1)

            def values(b):
                blk = BLOCKS[b]
                last_unit = blk["units"][-1]
                if blk["diagonal"]:
                    pe.wait_ge(masked, MASKS_THROUGH[last_unit])
                else:
                    pe.wait_ge(exp_ready, last_unit + 1)
                if blk["first"]:
                    pe.wait_ge(v_ready, blk["c"] + 1)
                    group = blk["c"] * NG + blk["g"]
                    if group:
                        pe.wait_ge(o_free, group)
                what = pieces(blk["kind"])
                for i, (dk, q0, n, place) in enumerate(what):
                    for j in range(GH):
                        head = blk["g"] * GH + j
                        if blk["kind"] == "mid":
                            buf, at = last_unit, j * 2 * P
                        else:
                            buf, at = blk["units"][j // 2], (j % 2) * CH + place
                        ins = nc.tensor.matmul(po[32 * j:32 * j + DH + 1, q0:q0 + n], va[:, blk["kt"] + dk, head, :],
                                               pbuf[:, buf % NPB, at:at + n], start=blk["first"],
                                               stop=blk["last"] and i + 1 == len(what), skip_group_check=True)
                ins.then_inc(block_done, 1)

            def job(n):
                name, c = JOBS[n]
                if name == "W":
                    return
                pe.wait_ge(job_fed, PRODUCTS[n])
                tile = lambda t: slice(t * P, (t + 1) * P)
                if name in ("T", "A", "X"):
                    src = {"T": xn, "A": att, "X": xn}[name]
                    for t in range(TC):
                        ins = nc.tensor.transpose(pm[:, tile(t)], src[:, t, :], idf[:, :])
                elif name in ("Q", "QS", "K", "KS"):
                    which = ("Q", "QS", "K", "KS").index(name)
                    ins = nc.tensor.matmul(pm[:, :], wqkv[:, which, :], xnT[:, :], start=True, stop=True)
                elif name == "V":
                    for t in range(TC):
                        ins = nc.tensor.matmul(pm[:, tile(t)], xnT[:, tile(t)], wqkv[:, 4, :], start=True, stop=True)
                elif name == "B":
                    ins = nc.tensor.matmul(pm[0:1, 0:H], bnd[:, :], hsum[:, :], start=True, stop=True)
                elif name[0] == "N":
                    pe.wait_ge(o_free, (c + 1) * NG)
                    t = int(name[1])
                    for g in range(NG):
                        ins = nc.tensor.transpose(pm[:, g * P:(g + 1) * P], oT[:, c % 2, g, tile(t)], idf[:, :])
                elif name == "O":
                    pe.wait_ge(ffn_in, 16 * 5)
                    for t in range(TC):
                        ins = nc.tensor.matmul(pm[:, tile(t)], xnT[:, tile(t)], wout[:, :], start=True, stop=True)
                elif name == "R":
                    for t in range(TC):
                        ins = nc.tensor.matmul(pm[:, t * P:t * P + RD + E], xnT[:, tile(t)], wdown[:, :],
                                               start=True, stop=True)
                elif name == "U":
                    for t in range(TC):
                        ins = nc.tensor.transpose(pm[0:RD + 1, tile(t)], low_rank[:, t, 0:RD + 1], idf[:, :])
                elif name == "F":
                    for t in range(TC):
                        nc.tensor.matmul(pm[:, tile(t)], xnT[:, tile(t)], wbase[:, :], start=True, stop=False)
                        ins = nc.tensor.matmul(pm[:, tile(t)], att[0:RD + 1, t, :], wup[:, :], start=False, stop=True)
                ins.then_inc(job_full, 1)

            def row_maxima(c):
                with pe.If(at_flag(pe, c) > 0):
                    if c:
                        pe.wait_ge(exp_ready, FIRST_UNIT[c])
                    for t in range(TC):
                        tile = c * TC + t
                        keys = (tile + 1) * P
                        with pe.Fori(0, NP) as pair:
                            for e in range(2):
                                if t == 0 and e == 0:
                                    with pe.If(pair > 0):
                                        pe.wait_ge(max_taken[c], pair * 2)
                                    pe.nop()
                                else:
                                    pe.wait_ge(max_taken[c], t * H + pair * 2 + e)
                                for k0 in range(0, keys, CH):
                                    n = min(CH, keys - k0)
                                    bank = k0 // CH
                                    edge = k0 + n == keys
                                    ins = nc.tensor.matmul(ps[:, bank // 2, bank % 2, 0:n],
                                                           qst[:, bass.ds(pair, 1), tile * P:(tile + 1) * P],
                                                           kst[:, bass.ds(pair * 2 + e, 1), k0:k0 + n],
                                                           start=True, stop=not edge, skip_group_check=True)
                                ins = nc.tensor.matmul(ps[:, bank // 2, bank % 2, n - P:n], idb[:, :], futb[:, :],
                                                       start=False, stop=True, skip_group_check=True)
                                ins.then_inc(max_scores[c], 1)
                    pe.wait_ge(max_taken[c], TC * H)
                    pe.wait_ge(max_vec[c], 1 + SHIFT_ROWS * (1 + TC) + SHIFT_ROWS - 1)
                    rows = 2 * SHIFT_ROWS * NP
                    for t in range(TC):
                        ins = nc.tensor.transpose(ps[0:rows, 0, 0, t * P:(t + 1) * P],
                                                  mparts[:, t, :, :, :].rearrange("p a b n -> p (a b n)"), idf[:, :])
                    ins.then_inc(max_scores[c], 1)
                    pe.wait_ge(max_stacked[c], 32)
                pe.nop()

            pe.wait_ge(const_in, 16 * 4)
            pe.wait_ge(qkv_in, 16)
            for n in range(len(PROJECT)):
                job(n)
            pe.wait_ge(ones_set, 7)
            due = {}
            for b, blk in enumerate(BLOCKS):
                due.setdefault(blk["units"][-1] + LAG, []).append(b)
            for u in range(len(UNITS)):
                if u in FIRST_UNIT:
                    c = FIRST_UNIT.index(u)
                    pe.wait_ge(stacked[c], 16 * 4 * len(SLOTS))
                    row_maxima(c)
                scores(u)
                for b in due.get(u, ()):
                    values(b)
                for n in JOBS_AT.get(u, ()):
                    job(n)
            for u in range(len(UNITS), len(UNITS) + LAG):
                for b in due.get(u, ()):
                    values(b)
            for n in TAIL_JOBS:
                job(n)


def rope_tables(order):
    inv = (np.float32(1.0) / np.float32(10000.0) ** (np.arange(0, DH, 2, dtype=np.float32) / np.float32(DH))).astype(np.float32)
    angle = (np.arange(S, dtype=np.float32)[:, None] * inv[None, :]).astype(np.float32)
    half = DH // 2
    d = order % DH
    cos, sin = np.cos(angle), np.sin(angle)
    sign = np.where(d < half, -1.0, 1.0).astype(np.float32)
    return np.ascontiguousarray(cos[:, d % half].T), np.ascontiguousarray((sin[:, d % half] * sign).T)


def kernel(L0_attn_x, L0_attn_w_qkv, L0_attn_w_out, L0_ffn_base_W, L0_ffn_base_b, L0_ffn_shared_A,
           L0_ffn_shared_B, L0_ffn_routed_A, L0_ffn_routed_B, L0_ffn_router_W, L0_ffn_router_b):
    from concourse import bacc
    from concourse.bass_utils import run_bass_kernel_spmd

    e, d, n = np.meshgrid(np.arange(2), np.arange(DH), np.arange(NP), indexing="ij")
    order = ((2 * n + e) * DH + d).reshape(-1)
    swapped = ((2 * n + e) * DH + (d + DH // 2) % DH).reshape(-1)
    w = np.asarray(L0_attn_w_qkv)
    w_q, w_k, w_v = w[:, :D], w[:, D:2 * D], w[:, 2 * D:]
    cos, sin = rope_tables(order)
    arrays = {
        "x": np.asarray(L0_attn_x).reshape(S, D),
        "w_qkv": np.stack([w_q[:, order], w_q[:, swapped], w_k[:, order], w_k[:, swapped], w_v], axis=1),
        "rope_c": cos,
        "rope_s": sin,
        "w_out": np.asarray(L0_attn_w_out),
        "w_down": np.concatenate([np.asarray(L0_ffn_shared_A), np.asarray(L0_ffn_routed_A).reshape(E * R, D),
                                  np.asarray(L0_ffn_router_W)]).T,
        "w_up": np.concatenate([np.asarray(L0_ffn_shared_B).T,
                                np.asarray(L0_ffn_routed_B).transpose(0, 2, 1).reshape(E * R, D),
                                np.asarray(L0_ffn_base_b)[None, :]]),
        "w_base": np.asarray(L0_ffn_base_W).T,
        "router_b": np.broadcast_to(np.asarray(L0_ffn_router_b)[None, :], (P, E)),
        "ident": np.eye(P, dtype=np.float32),
        "head_sum": (order[:, None] // DH == np.arange(H)[None, :]).astype(np.float32),
        "lower": np.broadcast_to(np.tril(np.ones((E, E), np.float32), -1)[None], (P, E, E)),
        "future": np.triu(np.full((P, P), MASKED, np.float32), 1),
    }
    arrays = {name: np.ascontiguousarray(a) for name, a in arrays.items()}
    nc = bacc.Bacc("TRN2", target_bir_lowering=False, num_devices=1)
    args = {name: nc.dram_tensor(f"{name}_dram", a.shape, F32, kind="ExternalInput").ap() for name, a in arrays.items()}
    out = nc.dram_tensor("out_dram", (S, D), F32, kind="ExternalOutput").ap()
    build(nc, **args, out=out)
    result = run_bass_kernel_spmd(nc, [{f"{name}_dram": a for name, a in arrays.items()}], core_ids=[0])
    return result.results[0]["out_dram"].reshape(1, S, D)
```

```python
from contextlib import ExitStack

import concourse.bass as bass
import numpy as np
from concourse import mybir

F32 = mybir.dt.float32
BF16 = mybir.dt.bfloat16
I32 = mybir.dt.int32
ALU = mybir.AluOpType
ACT = mybir.ActivationFunctionType
AX = mybir.AxisListType

P = 128
S = 2048
D = 128
H = 16
DH = D // H
NP = H // 2
CH = 512
NC = S // CH
TC = CH // P
NT = S // P
GH = 4
NG = H // GH
E, R = 6, 16
RD = R + E * R
SCALE = DH ** -0.5
EPS = 1e-5
BOUND = 60.0
MASKED = -3.0e38

SLOTS = ((0, 0), (0, 1), (1, 0), (1, 1), (0, 2), (2, 0))
SHIFT = 2 * DH * len(SLOTS)
SHIFT_ROWS = 3
KDMAS, QDMAS, ODMAS = 2 * len(SLOTS), len(SLOTS), 2

NS = 3
NPB = 7
LAG = 5


def plan():
    units, blocks = [], []
    for c in range(NC):
        for g in range(NG):
            work = [("full", kt) for kt in range(4 * c + 1)] + [("ends", 4 * c + 1), ("mid", 4 * c + 2)]
            for n, (kind, kt) in enumerate(work):
                diagonal = kt >= 4 * c
                mine = []
                for pair in ((0, 1),) if kind == "mid" else ((0,), (1,)):
                    mine.append(len(units))
                    units.append(dict(c=c, g=g, kind=kind, kt=kt, pairs=pair, diagonal=diagonal, block=len(blocks)))
                blocks.append(dict(c=c, g=g, kind=kind, kt=kt, units=mine, first=n == 0,
                                   last=n == len(work) - 1, diagonal=diagonal))
    return units, blocks


UNITS, BLOCKS = plan()
MASKS_THROUGH = [sum(u["diagonal"] for u in UNITS[:n + 1]) for n in range(len(UNITS))]
FIRST_UNIT = [next(n for n, u in enumerate(UNITS) if u["c"] == c) for c in range(NC)]


def pieces(unit_kind):
    return {"full": [(0, 0, CH, 0)],
            "ends": [(0, P, CH - P, 0), (2, CH - P, P, CH - P)],
            "mid": [(0, 2 * P, 2 * P, 0)]}[unit_kind]


PROJECT = ("T", "K", "KS", "Q", "QS", "V", "B")
FINISH = ("N0", "N1", "A", "O", "X", "R", "W", "U", "F")
ROOM = {"T": 1.2, "K": 1.4, "KS": 4.5, "Q": 1.4, "QS": 5.0, "V": 1.6, "B": 5.0,
        "N0": 1.6, "N1": 1.6, "A": 1.4, "O": 5.5, "X": 1.4, "R": 4.0, "W": 5.0, "U": 1.4, "F": 6.0}


def schedule():
    jobs = [(name, 0) for name in PROJECT]
    at = {}
    for c in range(NC):
        begin = FIRST_UNIT[c]
        end = FIRST_UNIT[c + 1] if c + 1 < NC else len(UNITS)
        todo = [(name, c + 1) for name in PROJECT] if c + 1 < NC else []
        todo += [(name, c - 1) for name in FINISH] if c else []
        at_unit = begin + (LAG + 2 if c else 1)
        spare = (end - 8 - at_unit) - sum(ROOM[name] for name, _ in todo)
        more = max(0.0, spare) / max(1, len(todo)) if c else 0.0
        for n, job in enumerate(todo):
            at.setdefault(min(int(at_unit), end - 1), []).append(len(jobs))
            at_unit += ROOM[job[0]] + more
            jobs.append(job)
    tail = list(range(len(jobs), len(jobs) + len(FINISH)))
    jobs += [(name, NC - 1) for name in FINISH]
    return jobs, at, tail


JOBS, JOBS_AT, TAIL_JOBS = schedule()
JOB = {job: n for n, job in enumerate(JOBS)}
PRODUCTS = [sum(name != "W" for name, _ in JOBS[:n + 1]) for n in range(len(JOBS))]
FIRST_JOBS = len(PROJECT)


def build(nc, x, w_qkv, rope_c, rope_s, w_out, w_down, w_up, w_base, router_b, ident, head_sum,
          pick_sums, lower, future, out):
    x_t = x.rearrange("(n p) d -> p n d", p=P)
    out_t = out.rearrange("(n p) d -> p n d", p=P)
    with ExitStack() as ctx:
        def sb(name, shape, dt=F32):
            return ctx.enter_context(nc.sbuf_tensor(name, shape, dt))

        def sem(name):
            return ctx.enter_context(nc.semaphore(name))

        wqkv = sb("wqkv", [P, 5, D])
        wout = sb("wout", [P, D])
        wdown = sb("wdown", [P, RD + E])
        wup = sb("wup", [RD + 1, D])
        wbase = sb("wbase", [P, D])
        rbias = sb("rbias", [P, E])
        idf = sb("idf", [P, P])
        idb = sb("idb", [P, P], BF16)
        hsum = sb("hsum", [P, H])
        pick = sb("pick", [P, GH * (DH + 1)])
        ones = sb("ones", [SHIFT_ROWS * NP, CH], BF16)
        low = sb("low", [P, E, E])
        fut = sb("fut", [P, P])
        futb = sb("futb", [P, P], BF16)
        cosT = sb("cosT", [P, 2, CH])
        sinT = sb("sinT", [P, 2, CH])
        xs = sb("xs", [P, NT, D])
        kst = sb("kst", [P, H, S], BF16)
        qst = sb("qst", [P, NP, S], BF16)
        va = sb("va", [P, NT, H, DH + 1])
        pbuf = sb("pbuf", [P, NPB, 2 * CH])
        oT = sb("oT", [P, 2, NG, CH])
        xn = sb("xn", [P, TC, D])
        xnT = sb("xnT", [P, CH])
        rot = sb("rot", [P, 2, CH])
        rest = sb("rest", [P, 2, CH])
        parts = sb("parts", [P, 2, 3, CH], BF16)
        stats = sb("stats", [P, TC, 6])
        mv = sb("mv", [P, TC, 2])
        var = sb("var", [P, TC])
        rstd = sb("rstd", [P, TC])
        sq = sb("sq", [P, TC])
        absmax = sb("absmax", [P, 2])
        kmax = sb("kmax", [P, 1])
        bnd = sb("bnd", [P, 1])
        bmax = sb("bmax", [1, 1])
        flag = sb("flag", [1, NC], I32)
        rec = sb("rec", [P, 2, H])
        att = sb("att", [P, TC, D])
        x1 = sb("x1", [P, TC, D])
        low_rank = sb("low_rank", [P, TC, P])
        lg = sb("lg", [P, TC, E])
        small = sb("small", [P, TC])
        gate = sb("gate", [P, TC, E])
        above = sb("above", [P, TC, E, E])
        ties = sb("ties", [P, TC, E, E])
        rank = sb("rank", [P, TC, E])
        rmax = sb("rmax", [P, TC, H])
        mparts = sb("mparts", [P, TC, 2, SHIFT_ROWS, NP])
        mrest = sb("mrest", [P, TC, H])
        mbf = sb("mbf", [P, TC, H], BF16)
        mrow = sb("mrow", [2 * SHIFT_ROWS * NP, CH], BF16)

        ps = ctx.enter_context(nc.psum_tensor("ps", [P, NS, 2, CH], F32))
        po = ctx.enter_context(nc.psum_tensor("po", [P, CH], F32))
        pm = ctx.enter_context(nc.psum_tensor("pm", [P, CH], F32))

        def bank(n):
            name, c = JOBS[n]
            if n < FIRST_JOBS and name in ("K", "KS", "Q", "QS", "V"):
                at = ("K", "KS", "Q", "QS", "V").index(name)
                return ps[:, at // 2, at % 2, :]
            if n == TAIL_JOBS[1]:
                return ps[:, 0, 0, :]
            return pm[:, :]

        def fed(n):
            if n < FIRST_JOBS and JOBS[n][0] in ("K", "KS", "Q", "QS", "V"):
                return 2
            if n == TAIL_JOBS[1]:
                return PRODUCTS[n - 1]
            return PRODUCTS[n]

        x_in = [sem(f"x_in{c}") for c in range(NC)]
        rope_in = [sem(f"rope_in{c}") for c in range(NC)]
        qkv_in, const_in, ffn_in = sem("qkv_in"), sem("const_in"), sem("ffn_in")
        zeroed = sem("zeroed")
        ones_set = sem("ones_set")
        ones_row = sem("ones_row")
        vec = sem("vec")
        parts_ready = sem("parts_ready")
        stacked = [sem(f"stacked{c}") for c in range(NC)]
        first_queries = sem("first_queries")
        v_ready = sem("v_ready")
        flag_ready = sem("flag_ready")
        job_fed = sem("job_fed")
        job_full = sem("job_full")
        scores_ready = sem("scores_ready")
        exp_ready = sem("exp_ready")
        masked = sem("masked")
        block_done = sem("block_done")
        o_free = sem("o_free")
        logits_ready = sem("logits_ready")
        logits_exp = sem("logits_exp")
        y_ready = sem("y_ready")
        stored = sem("stored")
        max_scores = [sem(f"max_scores{c}") for c in range(NC)]
        max_taken = [sem(f"max_taken{c}") for c in range(NC)]
        max_vec = [sem(f"max_vec{c}") for c in range(NC)]
        max_rows = [sem(f"max_rows{c}") for c in range(NC)]
        max_stacked = [sem(f"max_stacked{c}") for c in range(NC)]

        ybuf = sb("ybuf", [P, TC, D])
        block = ctx.enter_context(nc.Block())

        def at_flag(engine, c):
            engine.wait_ge(flag_ready, c + 1)
            return engine.value_load(flag[0:1, c:c + 1], min_val=0, max_val=1)

        def stack_ones(engine, c):
            engine.wait_ge(zeroed, c + 1)
            engine.wait_ge(ones_row, 1)
            for e in range(2):
                row = SHIFT + e * SHIFT_ROWS
                engine.dma_start(kst[row:row + SHIFT_ROWS, e::2, c * CH:(c + 1) * CH], ones[:, :]).then_inc(stacked[c], 16)

        def stack_keys(engine, c):
            engine.wait_ge(parts_ready, 2 * c + 1)
            engine.wait_ge(zeroed, c + 1)
            for r, (part, _) in enumerate(SLOTS):
                for e in range(2):
                    row = (2 * r + e) * DH
                    engine.dma_start(kst[row:row + DH, e::2, c * CH:(c + 1) * CH],
                                     parts[e * DH * NP:(e + 1) * DH * NP, 0, part, :]).then_inc(stacked[c], 16)

        def stack_queries(engine, c):
            engine.wait_ge(parts_ready, 2 * c + 2)
            engine.wait_ge(zeroed, c + 1)
            for r, (_, part) in enumerate(SLOTS):
                row = 2 * r * DH
                engine.dma_start(qst[row:row + 2 * DH, :, c * CH:(c + 1) * CH],
                                 parts[:, 1, part, :]).then_inc(stacked[c] if c else first_queries, 16)

        def wait_stacked(engine, c):
            engine.wait_ge(stacked[c], 16 * (KDMAS + ODMAS + (QDMAS if c else 0)))
            if c == 0:
                engine.wait_ge(first_queries, 16 * QDMAS)

        @block.sync
        def _(sp):
            def load_chunk(c):
                cols = slice(c * CH, (c + 1) * CH)
                sp.dma_start(xs[:, c * TC:(c + 1) * TC, :], x_t[:, c * TC:(c + 1) * TC, :]).then_inc(x_in[c], 16)
                if c == 0:
                    sp.dma_start(idf[:, :], ident).then_inc(const_in, 16)
                    sp.dma_start(wqkv[:, :, :], w_qkv).then_inc(qkv_in, 16)
                sp.dma_start(cosT[:, c % 2, :], rope_c[:, cols]).then_inc(rope_in[c], 16)
                sp.dma_start(sinT[:, c % 2, :], rope_s[:, cols]).then_inc(rope_in[c], 16)

            def stack_maxima(c):
                with sp.If(at_flag(sp, c) > 0):
                    sp.wait_ge(max_rows[c], 1)
                    sp.dma_start(qst[SHIFT:SHIFT + 2 * SHIFT_ROWS, :, c * CH:(c + 1) * CH],
                                 mrow[:, :]).then_inc(max_stacked[c], 16)
                    sp.wait_ge(max_stacked[c], 16)

            def store(c):
                sp.wait_ge(y_ready, c + 1)
                sp.dma_start(out_t[:, c * TC:(c + 1) * TC, :], ybuf[:, :, :]).then_inc(stored, 16)

            load_chunk(0)
            sp.dma_start(hsum[:, :], head_sum).then_inc(const_in, 16)
            sp.dma_start(fut[:, :], future).then_inc(const_in, 16)
            sp.dma_start(low[:, :, :], lower).then_inc(const_in, 16)
            sp.dma_start(pick[:, :], pick_sums).then_inc(const_in, 16)
            stack_ones(sp, 0)
            stack_keys(sp, 0)
            load_chunk(1)
            for dst, src in ((wout, w_out), (wdown, w_down), (wup, w_up), (wbase, w_base), (rbias, router_b)):
                sp.dma_start(dst[:, :], src).then_inc(ffn_in, 16)
            stack_maxima(0)
            for c in range(1, NC):
                stack_ones(sp, c)
                stack_keys(sp, c)
                stack_queries(sp, c)
                if c + 1 < NC:
                    load_chunk(c + 1)
                if c >= 2:
                    store(c - 2)
                stack_maxima(c)
            store(NC - 2)
            store(NC - 1)
            sp.wait_ge(stored, 16 * NC)

        @block.gpsimd
        def _(pool):
            nc.gpsimd.memset(ones[:, :], 1.0).then_inc(ones_row, 1)
            for c in range(NC):
                words = slice(c * CH // 2, (c + 1) * CH // 2)
                nc.gpsimd.memset(qst[:, :, :].bitcast(F32)[:, :, words], 0.0)
                nc.gpsimd.memset(kst[:, :, :].bitcast(F32)[:, :, words], 0.0).then_inc(zeroed, 1)
                if c == 0:
                    stack_queries(pool, 0)
            for u, unit in enumerate(UNITS):
                if not unit["diagonal"]:
                    continue
                pool.wait_ge(exp_ready, u + 1)
                buf = pbuf[:, u % NPB, :]
                if unit["kind"] == "mid":
                    edges = [buf.rearrange("p (h q) -> p h q", h=4)[:, :, 0:P]]
                else:
                    heads = buf.rearrange("p (h q) -> p h q", h=2)
                    edges = [heads[:, :, place:place + P] for _, _, _, place in pieces(unit["kind"])]
                for edge in edges:
                    ins = nc.gpsimd.affine_select(out=edge, in_=edge, compare_op=ALU.is_ge, fill=0.0, base=0,
                                                  pattern=[[0, edge.shape[1]], [1, P]], channel_multiplier=-1)
                ins.then_inc(masked, 1)

        @block.scalar
        def _(act):
            for u, unit in enumerate(UNITS):
                act.wait_ge(scores_ready, u + 1)
                if u >= NPB:
                    act.wait_ge(block_done, UNITS[u - NPB]["block"] + 1)
                nc.scalar.activation(pbuf[:, u % NPB, :], ps[:, u % NS, :, :].rearrange("p b q -> p (b q)"),
                                     ACT.Exp, scale=SCALE).then_inc(exp_ready, 1)
                for n in JOBS_AT.get(u, ()):
                    if JOBS[n][0] == "R":
                        act.wait_ge(logits_ready, JOBS[n][1] + 1)
                        nc.scalar.activation(gate[:, :, :], lg[:, :, :], ACT.Exp).then_inc(logits_exp, 1)
            act.wait_ge(logits_ready, NC)
            nc.scalar.activation(gate[:, :, :], lg[:, :, :], ACT.Exp).then_inc(logits_exp, 1)

        @block.vector
        def _(dve):
            steps = [0]

            def then(ins):
                steps[0] += 1
                ins.then_inc(vec, 1)
                dve.wait_ge(vec, steps[0])

            def inverse_sqrt():
                then(nc.vector.tensor_scalar(var[:, :], mv[:, :, 1], EPS, None, ALU.add))
                then(nc.vector.tensor_scalar(rstd[:, :].bitcast(I32), var[:, :].bitcast(I32), -0.5, float(0x5F3759DF),
                                             ALU.mult, ALU.add))
                for _ in range(3):
                    then(nc.vector.tensor_tensor(sq[:, :], rstd[:, :], rstd[:, :], ALU.mult))
                    then(nc.vector.scalar_tensor_tensor(sq[:, :], sq[:, :], -0.5, var[:, :], ALU.mult, ALU.mult))
                    then(nc.vector.scalar_tensor_tensor(rstd[:, :], sq[:, :], 1.5, rstd[:, :], ALU.add, ALU.mult))

            def layernorm(src):
                for t in range(TC):
                    ins = nc.vector.bn_stats(stats[:, t, :], src(t))
                then(ins)
                for t in range(TC):
                    ins = nc.vector.bn_aggr(mv[:, t, :], stats[:, t, :])
                then(ins)
                inverse_sqrt()
                for t in range(TC):
                    ins = nc.vector.tensor_scalar(xn[:, t, :], src(t), mv[:, t, 0:1], rstd[:, t:t + 1],
                                                  ALU.subtract, ALU.mult)
                then(ins)

            def evacuate(block_index):
                b = BLOCKS[block_index]
                dve.wait_ge(block_done, block_index + 1)
                nc.vector.tensor_copy(oT[:, b["c"] % 2, b["g"], :], po[:, :]).then_inc(o_free, 1)

            def rotate(which, c, product, swapped):
                if not swapped:
                    dve.wait_ge(rope_in[c], 32)
                    then(nc.vector.tensor_tensor(rot[:, which, :], product, cosT[:, c % 2, :], ALU.mult))
                else:
                    then(nc.vector.tensor_tensor(rest[:, which, :], product, sinT[:, c % 2, :], ALU.mult))
                    then(nc.vector.tensor_tensor(rot[:, which, :], rot[:, which, :], rest[:, which, :], ALU.add))

            def split(which, c):
                if c:
                    wait_stacked(dve, c - 1)
                whole, left, part = rot[:, which, :], rest[:, which, :], parts[:, which, :, :]
                then(nc.vector.tensor_copy(part[:, 0, :], whole))
                then(nc.vector.tensor_tensor(left, whole, part[:, 0, :], ALU.subtract))
                then(nc.vector.tensor_copy(part[:, 1, :], left))
                nc.vector.tensor_tensor(part[:, 2, :], left, part[:, 1, :], ALU.subtract).then_inc(parts_ready, 1)

            def bound(c):
                then(nc.vector.tensor_reduce(absmax[:, :], rot[:, :, :], AX.X, ALU.max, apply_absolute_value=True))
                if c:
                    then(nc.vector.tensor_tensor(kmax[:, :], kmax[:, :], absmax[:, 0:1], ALU.max))
                else:
                    then(nc.vector.tensor_copy(kmax[:, :], absmax[:, 0:1]))
                then(nc.vector.tensor_tensor(bnd[:, :], absmax[:, 1:2], kmax[:, :], ALU.mult))

            def choose():
                shape = [P, TC, E, E]
                this, other = (gate[:, :, :].unsqueeze(3).broadcast_to(shape), gate[:, :, :].unsqueeze(2).broadcast_to(shape))
                per_token = small[:, :].unsqueeze(2).broadcast_to([P, TC, E])
                then(nc.vector.tensor_reduce(small[:, :], gate[:, :, :], AX.X, ALU.add))
                then(nc.vector.reciprocal(small[:, :], small[:, :]))
                then(nc.vector.tensor_tensor(gate[:, :, :], gate[:, :, :], per_token, ALU.mult))
                nc.vector.tensor_tensor(above[:, :, :, :], other, this, ALU.is_gt)
                then(nc.vector.tensor_tensor(ties[:, :, :, :], other, this, ALU.is_equal))
                then(nc.vector.tensor_tensor(ties[:, :, :, :], ties[:, :, :, :],
                                             low[:, :, :].unsqueeze(1).broadcast_to(shape), ALU.mult))
                then(nc.vector.tensor_tensor(above[:, :, :, :], above[:, :, :, :], ties[:, :, :, :], ALU.add))
                then(nc.vector.tensor_reduce(rank[:, :, :], above[:, :, :, :], AX.X, ALU.add))
                then(nc.vector.scalar_tensor_tensor(gate[:, :, :], rank[:, :, :], 1.5, gate[:, :, :], ALU.is_lt, ALU.mult))
                then(nc.vector.tensor_reduce(small[:, :], gate[:, :, :], AX.X, ALU.add))
                then(nc.vector.tensor_scalar(small[:, :], small[:, :], 1e-6, None, ALU.add))
                then(nc.vector.reciprocal(small[:, :], small[:, :]))
                then(nc.vector.tensor_tensor(gate[:, :, :], gate[:, :, :], per_token, ALU.mult))

            def take(n):
                name, c = JOBS[n]
                if name != "W":
                    dve.wait_ge(job_full, PRODUCTS[n])
                tiles = slice(c * TC, (c + 1) * TC)
                product = bank(n)
                by_tile = product.rearrange("p (t d) -> p t d", t=TC)
                if name in ("T", "A", "X"):
                    then(nc.vector.tensor_copy(xnT[:, :], product))
                elif name in ("K", "KS", "Q", "QS"):
                    which = 0 if name[0] == "K" else 1
                    rotate(which, c, product, len(name) == 2)
                    if len(name) == 2:
                        split(which, c)
                    if name == "QS":
                        bound(c)
                elif name == "V":
                    nc.vector.tensor_copy(va[:, tiles, :, 0:DH],
                                          product.rearrange("p (t h d) -> p t h d", t=TC, h=H)).then_inc(v_ready, 1)
                    dve.wait_ge(v_ready, c + 1)
                elif name == "B":
                    then(nc.vector.tensor_reduce(bmax[:, :], product[0:1, 0:H], AX.X, ALU.max))
                    nc.vector.tensor_scalar(flag[0:1, c:c + 1], bmax[:, :], BOUND / SCALE, None,
                                            ALU.is_gt).then_inc(flag_ready, 1)
                elif name[0] == "N":
                    two = slice(2 * int(name[1]), 2 * int(name[1]) + 2)
                    heads = product[:, 0:2 * H * (DH + 1)].rearrange("p (t h d) -> p t h d", t=2, h=H)
                    then(nc.vector.reciprocal(rec[:, :, :], heads[:, :, :, DH]))
                    then(nc.vector.tensor_tensor(att[:, two, :].rearrange("p t (h d) -> p t h d", h=H),
                                                 heads[:, :, :, 0:DH],
                                                 rec[:, :, :].unsqueeze(3).broadcast_to([P, 2, H, DH]), ALU.mult))
                elif name == "O":
                    then(nc.vector.tensor_tensor(x1[:, :, :], by_tile, xs[:, tiles, :], ALU.add))
                    layernorm(lambda t: x1[:, t, :])
                elif name == "R":
                    dve.wait_ge(ffn_in, 16 * 5)
                    nc.vector.tensor_copy(low_rank[:, :, 0:RD], by_tile[:, :, 0:RD])
                    then(nc.vector.tensor_tensor(lg[:, :, :], by_tile[:, :, RD:RD + E],
                                                 rbias[:, :].unsqueeze(1).broadcast_to([P, TC, E]), ALU.add))
                    then(nc.vector.tensor_reduce(small[:, :], lg[:, :, :], AX.X, ALU.max))
                    nc.vector.tensor_tensor(lg[:, :, :], lg[:, :, :], small[:, :].unsqueeze(2).broadcast_to([P, TC, E]),
                                            ALU.subtract).then_inc(logits_ready, 1)
                elif name == "W":
                    dve.wait_ge(logits_exp, c + 1)
                    choose()
                    routed = low_rank[:, :, R:RD].rearrange("p t (e r) -> p t e r", e=E)
                    then(nc.vector.tensor_tensor(routed, routed,
                                                 gate[:, :, :].unsqueeze(3).broadcast_to([P, TC, E, R]), ALU.mult))
                elif name == "U":
                    then(nc.vector.tensor_copy(att[0:RD + 1, :, :].rearrange("p t d -> p (t d)"), product[0:RD + 1, :]))
                elif name == "F":
                    if c:
                        dve.wait_ge(stored, 16 * c)
                    nc.vector.tensor_tensor(ybuf[:, :, :], by_tile, x1[:, :, :], ALU.add).then_inc(y_ready, 1)
                    dve.wait_ge(y_ready, c + 1)
                if n + 1 < len(JOBS) and JOBS[n + 1][0] == "T":
                    normalise(JOBS[n + 1][1])
                if n + 1 < len(JOBS) and JOBS[n + 1][0] != "W":
                    nc.vector.engine_nop().then_inc(job_fed, 1)

            def normalise(c):
                dve.wait_ge(x_in[c], 16)
                layernorm(lambda t: xs[:, c * TC + t, :])

            def row_maxima(c):
                with dve.If(at_flag(dve, c) > 0):
                    for t in range(TC):
                        width = (c * TC + t + 1) * P
                        with dve.Fori(0, NP) as pair:
                            for e in range(2):
                                dve.wait_ge(max_scores[c], t * H + pair * 2 + (e + 1))
                                nc.vector.tensor_reduce(
                                    rmax[:, t, bass.ds(pair * 2 + e, 1)],
                                    ps[:, :, :, :].rearrange("p a b q -> p (a b q)")[:, 0:width],
                                    AX.X, ALU.max).then_inc(max_taken[c], 1)
                    dve.wait_ge(max_taken[c], TC * H)
                    n = [0]

                    def after(ins):
                        n[0] += 1
                        ins.then_inc(max_vec[c], 1)
                        dve.wait_ge(max_vec[c], n[0])
                    after(nc.vector.tensor_scalar(mrest[:, :, :], rmax[:, :, :], -1.0, None, ALU.mult))
                    by_half = mbf[:, :, :].rearrange("p t (n e) -> p t e n", e=2)
                    for part in range(SHIFT_ROWS):
                        after(nc.vector.tensor_copy(mbf[:, :, :], mrest[:, :, :]))
                        for t in range(TC):
                            after(nc.vector.tensor_copy(mparts[:, t, :, part, :], by_half[:, t, :, :]))
                        if part + 1 < SHIFT_ROWS:
                            after(nc.vector.tensor_tensor(mrest[:, :, :], mrest[:, :, :], mbf[:, :, :], ALU.subtract))
                    dve.wait_ge(max_scores[c], TC * H + 1)
                    nc.vector.tensor_copy(mrow[:, :], ps[0:2 * SHIFT_ROWS * NP, 0, 0, :]).then_inc(max_rows[c], 1)
                    dve.wait_ge(max_rows[c], 1)
                nc.vector.engine_nop()

            nc.vector.memset(po[:, :], 0.0).then_inc(ones_set, 1)
            nc.vector.memset(va[:, :, :, DH:DH + 1], 1.0).then_inc(ones_set, 1)
            nc.vector.memset(low_rank[:, :, RD:P], 1.0).then_inc(ones_set, 1)
            normalise(0)
            nc.vector.engine_nop().then_inc(job_fed, 1)
            for n in range(len(PROJECT)):
                take(n)
                if n == 0:
                    dve.wait_ge(const_in, 16 * 5)
                    nc.vector.tensor_copy(idb[:, :], idf[:, :]).then_inc(ones_set, 1)
                    nc.vector.tensor_copy(futb[:, :], fut[:, :]).then_inc(ones_set, 1)
            row_maxima(0)
            ends = {b["units"][-1] + LAG: n for n, b in enumerate(BLOCKS) if b["last"]}
            for u in range(len(UNITS)):
                if u in FIRST_UNIT[1:]:
                    row_maxima(FIRST_UNIT.index(u))
                if u in ends:
                    evacuate(ends[u])
                for n in JOBS_AT.get(u, ()):
                    take(n)
            evacuate(len(BLOCKS) - 1)
            for n in TAIL_JOBS:
                take(n)

        @block.tensor
        def _(pe):
            def scores(u):
                unit = UNITS[u]
                c, g, kt = unit["c"], unit["g"], unit["kt"]
                if u >= NS:
                    pe.wait_ge(exp_ready, u - NS + 1)
                per_pair = len(unit["pairs"])
                for at, pair in enumerate(unit["pairs"]):
                    for e in range(2):
                        head = g * GH + pair * 2 + e
                        for dk, q0, n, place in pieces(unit["kind"]):
                            bank = e if per_pair == 1 else at
                            place += 0 if per_pair == 1 else e * 2 * P
                            key = (kt + dk) * P
                            q = c * CH + q0
                            ins = nc.tensor.matmul(ps[:, u % NS, bank, place:place + n], kst[:, head, key:key + P],
                                                   qst[:, g * 2 + pair, q:q + n], start=True, stop=True)
                ins.then_inc(scores_ready, 1)

            def values(b):
                blk = BLOCKS[b]
                last_unit = blk["units"][-1]
                if blk["diagonal"]:
                    pe.wait_ge(masked, MASKS_THROUGH[last_unit])
                else:
                    pe.wait_ge(exp_ready, last_unit + 1)
                if blk["first"]:
                    pe.wait_ge(v_ready, blk["c"] + 1)
                    group = blk["c"] * NG + blk["g"]
                    if group:
                        pe.wait_ge(o_free, group)
                what = pieces(blk["kind"])
                for i, (dk, q0, n, place) in enumerate(what):
                    for j in range(GH):
                        head = blk["g"] * GH + j
                        if blk["kind"] == "mid":
                            buf, at = last_unit, j * 2 * P
                        else:
                            buf, at = blk["units"][j // 2], (j % 2) * CH + place
                        ins = nc.tensor.matmul(po[32 * j:32 * j + DH + 1, q0:q0 + n], va[:, blk["kt"] + dk, head, :],
                                               pbuf[:, buf % NPB, at:at + n], start=blk["first"],
                                               stop=blk["last"] and i + 1 == len(what), skip_group_check=True)
                ins.then_inc(block_done, 1)

            def job(n):
                name, c = JOBS[n]
                if name == "W":
                    return
                pe.wait_ge(job_fed, fed(n))
                product = bank(n)
                tile = lambda t: slice(t * P, (t + 1) * P)
                if name in ("T", "A", "X"):
                    src = {"T": xn, "A": att, "X": xn}[name]
                    for t in range(TC):
                        ins = nc.tensor.transpose(product[:, tile(t)], src[:, t, :], idf[:, :])
                elif name in ("K", "KS", "Q", "QS"):
                    which = ("K", "KS", "Q", "QS").index(name)
                    ins = nc.tensor.matmul(product, wqkv[:, which, :], xnT[:, :], start=True, stop=True)
                elif name == "V":
                    for t in range(TC):
                        ins = nc.tensor.matmul(product[:, tile(t)], xnT[:, tile(t)], wqkv[:, 4, :], start=True, stop=True)
                elif name == "B":
                    ins = nc.tensor.matmul(product[0:1, 0:H], bnd[:, :], hsum[:, :], start=True, stop=True)
                elif name[0] == "N":
                    pe.wait_ge(o_free, (c + 1) * NG)
                    width = GH * (DH + 1)
                    for i in range(2):
                        for g in range(NG):
                            at = (i * NG + g) * width
                            ins = nc.tensor.matmul(product[:, at:at + width], oT[:, c % 2, g, tile(2 * int(name[1]) + i)],
                                                   pick[:, :], start=True, stop=True)
                elif name == "O":
                    pe.wait_ge(ffn_in, 16 * 5)
                    for t in range(TC):
                        ins = nc.tensor.matmul(product[:, tile(t)], xnT[:, tile(t)], wout[:, :], start=True, stop=True)
                elif name == "R":
                    for t in range(TC):
                        ins = nc.tensor.matmul(product[:, t * P:t * P + RD + E], xnT[:, tile(t)], wdown[:, :],
                                               start=True, stop=True)
                elif name == "U":
                    for t in range(TC):
                        ins = nc.tensor.transpose(product[0:RD + 1, tile(t)], low_rank[:, t, 0:RD + 1], idf[:, :])
                elif name == "F":
                    for t in range(TC):
                        nc.tensor.matmul(product[:, tile(t)], xnT[:, tile(t)], wbase[:, :], start=True, stop=False)
                        ins = nc.tensor.matmul(product[:, tile(t)], att[0:RD + 1, t, :], wup[:, :], start=False, stop=True)
                ins.then_inc(job_full, 1)

            def row_maxima(c):
                with pe.If(at_flag(pe, c) > 0):
                    if c:
                        pe.wait_ge(exp_ready, FIRST_UNIT[c])
                    for t in range(TC):
                        tile = c * TC + t
                        keys = (tile + 1) * P
                        with pe.Fori(0, NP) as pair:
                            for e in range(2):
                                if t == 0 and e == 0:
                                    with pe.If(pair > 0):
                                        pe.wait_ge(max_taken[c], pair * 2)
                                    pe.nop()
                                else:
                                    pe.wait_ge(max_taken[c], t * H + pair * 2 + e)
                                for k0 in range(0, keys, CH):
                                    n = min(CH, keys - k0)
                                    bank = k0 // CH
                                    edge = k0 + n == keys
                                    ins = nc.tensor.matmul(ps[:, bank // 2, bank % 2, 0:n],
                                                           qst[:, bass.ds(pair, 1), tile * P:(tile + 1) * P],
                                                           kst[:, bass.ds(pair * 2 + e, 1), k0:k0 + n],
                                                           start=True, stop=not edge, skip_group_check=True)
                                ins = nc.tensor.matmul(ps[:, bank // 2, bank % 2, n - P:n], idb[:, :], futb[:, :],
                                                       start=False, stop=True, skip_group_check=True)
                                ins.then_inc(max_scores[c], 1)
                    pe.wait_ge(max_taken[c], TC * H)
                    pe.wait_ge(max_vec[c], 1 + SHIFT_ROWS * (1 + TC) + SHIFT_ROWS - 1)
                    rows = 2 * SHIFT_ROWS * NP
                    for t in range(TC):
                        ins = nc.tensor.transpose(ps[0:rows, 0, 0, t * P:(t + 1) * P],
                                                  mparts[:, t, :, :, :].rearrange("p a b n -> p (a b n)"), idf[:, :])
                    ins.then_inc(max_scores[c], 1)
                    pe.wait_ge(max_stacked[c], 16)
                pe.nop()

            pe.wait_ge(const_in, 16 * 5)
            pe.wait_ge(qkv_in, 16)
            for n in range(len(PROJECT)):
                job(n)
            pe.wait_ge(ones_set, 5)
            due = {}
            for b, blk in enumerate(BLOCKS):
                due.setdefault(blk["units"][-1] + LAG, []).append(b)
            for u in range(len(UNITS)):
                if u in FIRST_UNIT:
                    c = FIRST_UNIT.index(u)
                    wait_stacked(pe, c)
                    row_maxima(c)
                scores(u)
                for b in due.get(u, ()):
                    values(b)
                for n in JOBS_AT.get(u, ()):
                    job(n)
            for u in range(len(UNITS), len(UNITS) + LAG):
                for b in due.get(u, ()):
                    values(b)
            for n in TAIL_JOBS:
                job(n)


def rope_tables(order):
    inv = (np.float32(1.0) / np.float32(10000.0) ** (np.arange(0, DH, 2, dtype=np.float32) / np.float32(DH))).astype(np.float32)
    angle = (np.arange(S, dtype=np.float32)[:, None] * inv[None, :]).astype(np.float32)
    half = DH // 2
    d = order % DH
    cos, sin = np.cos(angle), np.sin(angle)
    sign = np.where(d < half, -1.0, 1.0).astype(np.float32)
    return np.ascontiguousarray(cos[:, d % half].T), np.ascontiguousarray((sin[:, d % half] * sign).T)


def kernel(L0_attn_x, L0_attn_w_qkv, L0_attn_w_out, L0_ffn_base_W, L0_ffn_base_b, L0_ffn_shared_A,
           L0_ffn_shared_B, L0_ffn_routed_A, L0_ffn_routed_B, L0_ffn_router_W, L0_ffn_router_b):
    from concourse import bacc
    from concourse.bass_utils import run_bass_kernel_spmd

    e, d, n = np.meshgrid(np.arange(2), np.arange(DH), np.arange(NP), indexing="ij")
    order = ((2 * n + e) * DH + d).reshape(-1)
    swapped = ((2 * n + e) * DH + (d + DH // 2) % DH).reshape(-1)
    w = np.asarray(L0_attn_w_qkv)
    w_q, w_k, w_v = w[:, :D], w[:, D:2 * D], w[:, 2 * D:]
    cos, sin = rope_tables(order)
    arrays = {
        "x": np.asarray(L0_attn_x).reshape(S, D),
        "w_qkv": np.stack([w_k[:, order], w_k[:, swapped], w_q[:, order], w_q[:, swapped], w_v], axis=1),
        "rope_c": cos,
        "rope_s": sin,
        "w_out": np.asarray(L0_attn_w_out),
        "w_down": np.concatenate([np.asarray(L0_ffn_shared_A), np.asarray(L0_ffn_routed_A).reshape(E * R, D),
                                  np.asarray(L0_ffn_router_W)]).T,
        "w_up": np.concatenate([np.asarray(L0_ffn_shared_B).T,
                                np.asarray(L0_ffn_routed_B).transpose(0, 2, 1).reshape(E * R, D),
                                np.asarray(L0_ffn_base_b)[None, :]]),
        "w_base": np.asarray(L0_ffn_base_W).T,
        "router_b": np.broadcast_to(np.asarray(L0_ffn_router_b)[None, :], (P, E)),
        "ident": np.eye(P, dtype=np.float32),
        "head_sum": (order[:, None] // DH == np.arange(H)[None, :]).astype(np.float32),
        "pick_sums": np.eye(P, dtype=np.float32).reshape(P, GH, P // GH)[:, :, :DH + 1].reshape(P, -1),
        "lower": np.broadcast_to(np.tril(np.ones((E, E), np.float32), -1)[None], (P, E, E)),
        "future": np.triu(np.full((P, P), MASKED, np.float32), 1),
    }
    arrays = {name: np.ascontiguousarray(a) for name, a in arrays.items()}
    nc = bacc.Bacc("TRN2", target_bir_lowering=False, num_devices=1)
    args = {name: nc.dram_tensor(f"{name}_dram", a.shape, F32, kind="ExternalInput").ap() for name, a in arrays.items()}
    out = nc.dram_tensor("out_dram", (S, D), F32, kind="ExternalOutput").ap()
    build(nc, **args, out=out)
    result = run_bass_kernel_spmd(nc, [{f"{name}_dram": a for name, a in arrays.items()}], core_ids=[0])
    return result.results[0]["out_dram"].reshape(1, S, D)
```

```python
from contextlib import ExitStack

import concourse.bass as bass
import numpy as np
from concourse import mybir

F32 = mybir.dt.float32
BF16 = mybir.dt.bfloat16
I32 = mybir.dt.int32
ALU = mybir.AluOpType
ACT = mybir.ActivationFunctionType
AX = mybir.AxisListType

P = 128
S = 2048
D = 128
H = 16
DH = D // H
NP = H // 2
HALF = NP * DH // 2
CH = 512
NC = S // CH
TC = CH // P
NT = S // P
GH = 4
NG = H // GH
E, R = 6, 16
RD = R + E * R
SCALE = DH ** -0.5
EPS = 1e-5
BOUND = 60.0
MASKED = -3.0e38
ONE_ONE = float(np.array([0x3F803F80], np.uint32).view(np.float32)[0])

SLOTS = ((0, 0), (0, 1), (1, 0), (1, 1), (0, 2), (2, 0))
SHIFT = 2 * DH * len(SLOTS)
SHIFT_ROWS = 3
ROWS = SHIFT + 2 * SHIFT_ROWS
K_ORDER = sorted((part, slot) for slot, (part, _) in enumerate(SLOTS))
Q_ORDER = sorted((part, slot) for slot, (_, part) in enumerate(SLOTS))
BY_POOL_K = (2,)
BY_POOL_Q = (2, 4)

NS = 3
NPB = 7
LAG = 5


def plan():
    units, blocks = [], []
    for c in range(NC):
        for g in range(NG):
            work = [("full", kt) for kt in range(4 * c + 1)] + [("ends", 4 * c + 1), ("mid", 4 * c + 2)]
            for n, (kind, kt) in enumerate(work):
                diagonal = kt >= 4 * c
                mine = []
                for pair in ((0, 1),) if kind == "mid" else ((0,), (1,)):
                    mine.append(len(units))
                    units.append(dict(c=c, g=g, kind=kind, kt=kt, pairs=pair, diagonal=diagonal, block=len(blocks)))
                blocks.append(dict(c=c, g=g, kind=kind, kt=kt, units=mine, first=n == 0,
                                   last=n == len(work) - 1, diagonal=diagonal))
    return units, blocks


UNITS, BLOCKS = plan()
MASKS_THROUGH = [sum(u["diagonal"] for u in UNITS[:n + 1]) for n in range(len(UNITS))]
FIRST_UNIT = [next(n for n, u in enumerate(UNITS) if u["c"] == c) for c in range(NC)]
SECOND_GROUP = [next(n for n, u in enumerate(UNITS) if u["c"] == c and u["g"] == 1) for c in range(NC)]


def blocks_by_unit():
    due = {}
    for b, block in enumerate(BLOCKS):
        at = block["units"][-1] + LAG
        due.setdefault(min(at, FIRST_UNIT[1]) if block["c"] == 0 else at, []).append(b)
    return due


def pieces(unit_kind):
    return {"full": [(0, 0, CH, 0)],
            "ends": [(0, P, CH - P, 0), (2, CH - P, P, CH - P)],
            "mid": [(0, 2 * P, 2 * P, 0)]}[unit_kind]


SWAPPED_PRODUCTS = 2
FIRST_PROJECT = ("L", "T", "K", "KS", "KP", "Q", "QS", "QP", "B", "S0", "S1", "V")
PROJECT = ("L", "T", "K", "KS", "KP", "Q", "QS", "V", "QP", "B", "S0", "S1")
FINISH = ("N0", "N1", "N2", "N3", "A", "O", "M", "X", "R", "W", "U", "F")
NO_PRODUCT = ("L", "KP", "QP", "S0", "S1", "M", "W")
MAKES_INPUT = ("L", "QP", "M", "W")
EARLY_FINISH = FINISH[0:NG - 1]
WARM = {"N3": 3, "A": 4, "O": 3, "X": 22, "R": 3, "U": 19, "F": 3}
WARM_START = 18
WARM_PARTS = 7
PLACES = (
    (0, 4, 5, 6, 7, 8, 9, 9, 9, 15, 16, 18),
    (7, 7, 8, 12, 13, 18, 19, 25, 25, 28, 28, 29, 31, 33, 35, 36, 36, 42, 44, 50, 50, 51),
    (4, 10, 11, 12, 16, 20, 20, 26, 27, 27, 30, 31, 33, 35, 37, 40, 40, 47, 51, 56, 61, 68),
    (5, 7, 13, 19, 31, 34, 34, 48, 63, 65, 85, 92, 94, 102, 104),
)


def projections(c):
    return [(name, c) for name in (PROJECT if c else FIRST_PROJECT)
            if c < SWAPPED_PRODUCTS or name not in ("KS", "QS")]


def schedule():
    jobs = projections(0)
    first, at = len(jobs), {}
    for c, places in enumerate(PLACES):
        mine = (projections(c + 1) if c + 1 < NC else []) + [(name, c - 1) for name in FINISH if c]
        if c == NC - 1:
            mine += [(name, c) for name in EARLY_FINISH]
        assert len(mine) == len(places)
        for job, place in zip(mine, places):
            at.setdefault(FIRST_UNIT[c] + place, []).append(len(jobs))
            jobs.append(job)
    tail = list(range(len(jobs), len(jobs) + len(FINISH) - len(EARLY_FINISH)))
    jobs += [(name, NC - 1) for name in FINISH[len(EARLY_FINISH):]]
    return jobs, first, at, tail


JOBS, FIRST_JOBS, JOBS_AT, TAIL_JOBS = schedule()
IS_PRODUCT = [name not in NO_PRODUCT for name, _ in JOBS]
FEEDS = {max(m for m in range(n) if IS_PRODUCT[m] or JOBS[m][0] in MAKES_INPUT)
         for n in range(len(JOBS)) if IS_PRODUCT[n]}
PRODUCTS = [sum(IS_PRODUCT[:n + 1]) for n in range(len(JOBS))]


def build(nc, x, w_qkv, rope_c, rope_s, w_out, w_down, w_up, w_base, router_b, ident, head_sum,
          own_rows, lower, future, out):
    x_t = x.rearrange("(n p) d -> p n d", p=P)
    out_t = out.rearrange("(n p) d -> p n d", p=P)
    with ExitStack() as ctx:
        def sb(name, shape, dt=F32):
            return ctx.enter_context(nc.sbuf_tensor(name, shape, dt))

        def sem(name):
            return ctx.enter_context(nc.semaphore(name))

        wqkv = sb("wqkv", [P, 5, D])
        wout = sb("wout", [P, D])
        wdown = sb("wdown", [P, RD + E])
        wup = sb("wup", [RD + 1, D])
        wbase = sb("wbase", [P, D])
        rbias = sb("rbias", [P, E])
        idf = sb("idf", [P, P])
        idb = sb("idb", [P, P], BF16)
        hsum = sb("hsum", [P, H])
        own = sb("own", [P, 2])
        low = sb("low", [P, E, E])
        fut = sb("fut", [P, P])
        futb = sb("futb", [P, P], BF16)
        cosT = sb("cosT", [P, 2, CH])
        sinT = sb("sinT", [P, 2, CH])
        xs = sb("xs", [P, NT, D])
        kst = sb("kst", [P, H, S], BF16)
        kpair = sb("kpair", [P, NP, CH], BF16)
        qst = sb("qst", [P, NP, S], BF16)
        va = sb("va", [P, NT, H, DH + 1])
        pbuf = sb("pbuf", [P, NPB, 2 * CH])
        oT = sb("oT", [P, 2, NG, CH])
        xn = sb("xn", [P, TC, D])
        xnT = sb("xnT", [P, CH])
        rot = sb("rot", [P, 2, CH])
        rest = sb("rest", [P, 2, CH])
        parts = sb("parts", [P, 2, 3, CH], BF16)
        stats = sb("stats", [P, TC, 6])
        mv = sb("mv", [P, 2, TC, 2])
        var = sb("var", [P, 2, TC])
        rstd = sb("rstd", [P, 2, TC])
        sq = sb("sq", [P, 2, TC])
        absmax = sb("absmax", [P, 2])
        kmax = sb("kmax", [P, 1])
        bnd = sb("bnd", [P, 1])
        bmax = sb("bmax", [1, 1])
        flag = sb("flag", [1, NC], I32)
        rec = sb("rec", [P, TC, GH])
        att = sb("att", [P, TC, D])
        low_rank = sb("low_rank", [P, TC, P])
        lg = sb("lg", [P, TC, E])
        small = sb("small", [P, TC])
        chosen = sb("chosen", [P, TC])
        gate = sb("gate", [P, TC, E])
        above = sb("above", [P, TC, E, E])
        ties = sb("ties", [P, TC, E, E])
        rank = sb("rank", [P, TC, E])
        rmax = sb("rmax", [P, TC, H])
        mparts = sb("mparts", [P, TC, 2, SHIFT_ROWS, NP])
        mrest = sb("mrest", [P, TC, H])
        mbf = sb("mbf", [P, TC, H], BF16)
        mrow = sb("mrow", [2 * SHIFT_ROWS * NP, CH], BF16)

        ps = ctx.enter_context(nc.psum_tensor("ps", [P, NS, 2, CH], F32))
        po = ctx.enter_context(nc.psum_tensor("po", [P, CH], F32))
        pm = ctx.enter_context(nc.psum_tensor("pm", [P, CH], F32))

        def bank(n):
            name, c = JOBS[n]
            if c == 0 and name in ("K", "KS", "Q", "QS"):
                at = ("K", "KS", "Q", "QS").index(name)
                return ps[:, at // 2, at % 2, :]
            if n == TAIL_JOBS[-1]:
                return ps[:, 1, 0, :]
            return pm[:, :]

        def fed(n):
            if JOBS[n][1] == 0 and JOBS[n][0] in ("K", "KS", "Q", "QS"):
                return 2
            return PRODUCTS[n]

        x_in = [sem(f"x_in{c}") for c in range(NC)]
        rope_in = [sem(f"rope_in{c}") for c in range(NC)]
        ident_in, qkv_in, const_in, ffn_in = sem("ident_in"), sem("qkv_in"), sem("const_in"), sem("ffn_in")
        zeroed = sem("zeroed")
        ones_set = sem("ones_set")
        warm_ready = sem("warm_ready")
        vec = sem("vec")
        parts_ready = sem("parts_ready")
        keys_in = [sem(f"keys_in{c}") for c in range(NC)]
        queries_in = [sem(f"queries_in{c}") for c in range(NC)]
        moments_ready = sem("moments_ready")
        rstd_ready = sem("rstd_ready")
        pool_steps = sem("pool_steps")
        keys_by_pool = sem("keys_by_pool")
        queries_by_pool = sem("queries_by_pool")
        keys_ready = sem("keys_ready")
        v_ready = sem("v_ready")
        flag_ready = sem("flag_ready")
        job_fed = sem("job_fed")
        job_full = sem("job_full")
        scores_ready = sem("scores_ready")
        exp_ready = sem("exp_ready")
        masked = sem("masked")
        block_done = sem("block_done")
        o_free = sem("o_free")
        logits_ready = sem("logits_ready")
        logits_exp = sem("logits_exp")
        y_ready = sem("y_ready")
        stored = sem("stored")
        max_masks = [sem(f"max_masks{c}") for c in range(NC)]
        max_scores = [sem(f"max_scores{c}") for c in range(NC)]
        max_taken = [sem(f"max_taken{c}") for c in range(NC)]
        max_vec = [sem(f"max_vec{c}") for c in range(NC)]
        max_rows = [sem(f"max_rows{c}") for c in range(NC)]
        max_stacked = [sem(f"max_stacked{c}") for c in range(NC)]

        block = ctx.enter_context(nc.Block())

        def at_flag(engine, c):
            engine.wait_ge(flag_ready, c + 1)
            return engine.value_load(flag[0:1, c:c + 1], min_val=0, max_val=1)

        def norm_at(c):
            return 1 if c == 1 else 0

        def inverse_sqrt(engine, then, c):
            at = norm_at(c)
            v, r, s = var[:, at, :], rstd[:, at, :], sq[:, at, :]
            then(engine.tensor_scalar(v, mv[:, at, :, 1], EPS, None, ALU.add))
            then(engine.tensor_scalar(r.bitcast(I32), v.bitcast(I32), -0.5, float(0x5F3759DF), ALU.mult, ALU.add))
            for _ in range(3):
                then(engine.tensor_tensor(s, r, r, ALU.mult))
                if engine is nc.gpsimd:
                    then(engine.tensor_tensor(s, s, v, ALU.mult))
                    then(engine.tensor_scalar(s, s, -0.5, 1.5, ALU.mult, ALU.add))
                    then(engine.tensor_tensor(r, r, s, ALU.mult))
                else:
                    then(engine.scalar_tensor_tensor(s, s, -0.5, v, ALU.mult, ALU.mult))
                    then(engine.scalar_tensor_tensor(r, s, 1.5, r, ALU.add, ALU.mult))

        def key_slot(r):
            return kpair[2 * r * DH:2 * (r + 1) * DH, :, :]

        def query_slot(r, c):
            return qst[2 * r * DH:2 * (r + 1) * DH, :, c * CH:(c + 1) * CH]

        def wait_for_keys(engine, c):
            if c == 0:
                engine.wait_ge(keys_in[0], 16 * (len(SLOTS) - len(BY_POOL_K)))
                engine.wait_ge(keys_by_pool, 16 * len(BY_POOL_K))
            else:
                engine.wait_ge(keys_in[c], 16 * len(SLOTS))

        def wait_for_queries(engine, c):
            if c == 0:
                engine.wait_ge(queries_in[0], 16 * (len(SLOTS) - len(BY_POOL_Q)))
                engine.wait_ge(queries_by_pool, 16 * len(BY_POOL_Q))
            else:
                engine.wait_ge(queries_in[c], 16 * len(SLOTS))

        @block.sync
        def _(sp):
            def load_chunk(c):
                cols = slice(c * CH, (c + 1) * CH)
                sp.dma_start(xs[:, c * TC:(c + 1) * TC, :], x_t[:, c * TC:(c + 1) * TC, :]).then_inc(x_in[c], 16)
                if c == 0:
                    sp.dma_start(idf[:, :], ident).then_inc(ident_in, 16)
                    sp.dma_start(wqkv[:, :, :], w_qkv).then_inc(qkv_in, 16)
                sp.dma_start(cosT[:, c % 2, :], rope_c[:, cols]).then_inc(rope_in[c], 16)
                sp.dma_start(sinT[:, c % 2, :], rope_s[:, cols]).then_inc(rope_in[c], 16)

            def stack(c):
                if c:
                    sp.wait_ge(keys_ready, 2 * c)
                for n, (part, r) in enumerate(K_ORDER):
                    if c or n not in BY_POOL_K:
                        sp.wait_ge(parts_ready, 6 * c + part + 1)
                        sp.dma_start(key_slot(r), parts[:, 0, part, :]).then_inc(keys_in[c], 16)
                for n, (part, r) in enumerate(Q_ORDER):
                    if c or n not in BY_POOL_Q:
                        sp.wait_ge(parts_ready, 6 * c + 3 + part + 1)
                        sp.dma_start(query_slot(r, c), parts[:, 1, part, :]).then_inc(queries_in[c], 16)

            def stack_maxima(c):
                with sp.If(at_flag(sp, c) > 0):
                    sp.wait_ge(max_rows[c], 1)
                    sp.dma_start(qst[SHIFT:SHIFT + 2 * SHIFT_ROWS, :, c * CH:(c + 1) * CH],
                                 mrow[:, :]).then_inc(max_stacked[c], 16)
                    sp.wait_ge(max_stacked[c], 16)

            def store(c):
                sp.wait_ge(y_ready, c + 1)
                sp.dma_start(out_t[:, c * TC:(c + 1) * TC, :], xs[:, c * TC:(c + 1) * TC, :]).then_inc(stored, 16)

            load_chunk(0)
            load_chunk(1)
            for dst, src in ((own, own_rows), (hsum, head_sum), (fut, future)):
                sp.dma_start(dst[:, :], src).then_inc(const_in, 16)
            sp.dma_start(low[:, :, :], lower).then_inc(const_in, 16)
            stack(0)
            for dst, src in ((wout, w_out), (wdown, w_down), (wup, w_up), (wbase, w_base), (rbias, router_b)):
                sp.dma_start(dst[:, :], src).then_inc(ffn_in, 16)
            stack_maxima(0)
            for c in range(1, NC):
                stack(c)
                if 2 <= c + 1 < NC:
                    load_chunk(c + 1)
                if c >= 2:
                    store(c - 2)
                stack_maxima(c)
            store(NC - 2)
            store(NC - 1)
            sp.wait_ge(stored, 16 * NC)

        @block.gpsimd
        def _(pool):
            nc.gpsimd.memset(qst[SHIFT:ROWS, :, :].bitcast(F32), 0.0).then_inc(zeroed, 1)
            pool.wait_ge(zeroed, 1)
            nc.gpsimd.memset(va[:, :, :, DH:DH + 1], 1.0).then_inc(zeroed, 1)
            steps = [0]

            def then(ins):
                steps[0] += 1
                ins.then_inc(pool_steps, 1)
                pool.wait_ge(pool_steps, steps[0])

            pool.wait_ge(moments_ready, 1)
            inverse_sqrt(nc.gpsimd, then, 1)
            nc.gpsimd.engine_nop().then_inc(rstd_ready, 1)
            for n in BY_POOL_K:
                part, r = K_ORDER[n]
                pool.wait_ge(parts_ready, part + 1)
                nc.gpsimd.dma_start(key_slot(r), parts[:, 0, part, :]).then_inc(keys_by_pool, 16)
            for n in BY_POOL_Q:
                part, r = Q_ORDER[n]
                pool.wait_ge(parts_ready, 3 + part + 1)
                nc.gpsimd.dma_start(query_slot(r, 0), parts[:, 1, part, :]).then_inc(queries_by_pool, 16)
            for u, unit in enumerate(UNITS):
                if not unit["diagonal"]:
                    continue
                pool.wait_ge(exp_ready, u + 1)
                buf = pbuf[:, u % NPB, :]
                if unit["kind"] == "mid":
                    edges = [buf.rearrange("p (h q) -> p h q", h=4)[:, :, 0:P]]
                else:
                    heads = buf.rearrange("p (h q) -> p h q", h=2)
                    edges = [heads[:, :, place:place + P] for _, _, _, place in pieces(unit["kind"])]
                for edge in edges:
                    ins = nc.gpsimd.affine_select(out=edge, in_=edge, compare_op=ALU.is_ge, fill=0.0, base=0,
                                                  pattern=[[0, edge.shape[1]], [1, P]], channel_multiplier=-1)
                ins.then_inc(masked, 1)

        @block.scalar
        def _(act):
            for u, unit in enumerate(UNITS):
                act.wait_ge(scores_ready, u + 1)
                if u >= NPB:
                    act.wait_ge(block_done, UNITS[u - NPB]["block"] + 1)
                nc.scalar.activation(pbuf[:, u % NPB, :], ps[:, u % NS, :, :].rearrange("p b q -> p (b q)"),
                                     ACT.Exp, scale=SCALE).then_inc(exp_ready, 1)
                for n in JOBS_AT.get(u, ()):
                    if JOBS[n][0] == "R":
                        act.wait_ge(logits_ready, JOBS[n][1] + 1)
                        nc.scalar.activation(gate[:, :, :], lg[:, :, :], ACT.Exp).then_inc(logits_exp, 1)
            act.wait_ge(logits_ready, NC)
            nc.scalar.activation(gate[:, :, :], lg[:, :, :], ACT.Exp).then_inc(logits_exp, 1)

        @block.vector
        def _(dve):
            steps = [0]

            def then(ins):
                steps[0] += 1
                ins.then_inc(vec, 1)
                dve.wait_ge(vec, steps[0])

            def moments(c, again=False):
                for t in range(TC):
                    ins = nc.vector.bn_stats(stats[:, t, :], xs[:, c * TC + t, :])
                then(ins)
                for t in range(TC):
                    ins = nc.vector.bn_aggr(mv[:, norm_at(c), t, :], stats[:, t, :])
                if c == 1 and not again:
                    ins.then_inc(moments_ready, 1)
                else:
                    then(ins)

            def layernorm(c, again=False):
                at = norm_at(c)
                if c == 1 and not again:
                    dve.wait_ge(rstd_ready, 1)
                else:
                    inverse_sqrt(nc.vector, then, c)
                for t in range(TC):
                    ins = nc.vector.tensor_scalar(xn[:, t, :], xs[:, c * TC + t, :], mv[:, at, t, 0:1], rstd[:, at, t:t + 1],
                                                  ALU.subtract, ALU.mult)
                then(ins)

            def evacuate(block_index):
                b = BLOCKS[block_index]
                dve.wait_ge(block_done, block_index + 1)
                nc.vector.tensor_copy(oT[:, b["c"] % 2, b["g"], :], po[:, :]).then_inc(o_free, 1)

            def rotate(which, c, product, swapped):
                if not swapped:
                    dve.wait_ge(rope_in[c], 32)
                    then(nc.vector.tensor_tensor(rot[:, which, :], product, cosT[:, c % 2, :], ALU.mult))
                if swapped:
                    then(nc.vector.tensor_tensor(rest[:, which, :], product, sinT[:, c % 2, :], ALU.mult))
                elif c >= SWAPPED_PRODUCTS:
                    for here in range(0, P, HALF):
                        there = here ^ HALF
                        ins = nc.vector.tensor_tensor(rest[there:there + HALF, which, :], product[here:here + HALF, :],
                                                      sinT[here:here + HALF, c % 2, :], ALU.mult)
                    then(ins)

            def split(which, c):
                then(nc.vector.tensor_tensor(rot[:, which, :], rot[:, which, :], rest[:, which, :], ALU.add))
                if c:
                    wait_for_keys(dve, c - 1)
                    wait_for_queries(dve, c - 1)
                whole, left, part = rot[:, which, :], rest[:, which, :], parts[:, which, :, :]
                done = 6 * c + 3 * which
                nc.vector.tensor_copy(part[:, 0, :], whole).then_inc(parts_ready, 1)
                dve.wait_ge(parts_ready, done + 1)
                then(nc.vector.tensor_tensor(left, whole, part[:, 0, :], ALU.subtract))
                nc.vector.tensor_copy(part[:, 1, :], left).then_inc(parts_ready, 1)
                dve.wait_ge(parts_ready, done + 2)
                nc.vector.tensor_tensor(part[:, 2, :], left, part[:, 1, :], ALU.subtract).then_inc(parts_ready, 1)

            def bound(c):
                then(nc.vector.tensor_reduce(absmax[:, :], rot[:, :, :], AX.X, ALU.max, apply_absolute_value=True))
                if c:
                    then(nc.vector.tensor_tensor(kmax[:, :], kmax[:, :], absmax[:, 0:1], ALU.max))
                else:
                    then(nc.vector.tensor_copy(kmax[:, :], absmax[:, 0:1]))
                then(nc.vector.tensor_tensor(bnd[:, :], absmax[:, 1:2], kmax[:, :], ALU.mult))

            def choose():
                shape = [P, TC, E, E]
                this, other = (gate[:, :, :].unsqueeze(3).broadcast_to(shape), gate[:, :, :].unsqueeze(2).broadcast_to(shape))
                per_token = small[:, :].unsqueeze(2).broadcast_to([P, TC, E])
                then(nc.vector.tensor_tensor(ties[:, :, :, :], other, this, ALU.is_equal))
                nc.vector.tensor_reduce(small[:, :], gate[:, :, :], AX.X, ALU.add)
                then(nc.vector.tensor_tensor(ties[:, :, :, :], ties[:, :, :, :],
                                             low[:, :, :].unsqueeze(1).broadcast_to(shape), ALU.mult))
                then(nc.vector.tensor_tensor(above[:, :, :, :], other, this, ALU.is_gt))
                then(nc.vector.tensor_tensor(above[:, :, :, :], above[:, :, :, :], ties[:, :, :, :], ALU.add))
                then(nc.vector.tensor_reduce(rank[:, :, :], above[:, :, :, :], AX.X, ALU.add))
                then(nc.vector.scalar_tensor_tensor(gate[:, :, :], rank[:, :, :], 1.5, gate[:, :, :], ALU.is_lt, ALU.mult))
                then(nc.vector.tensor_reduce(chosen[:, :], gate[:, :, :], AX.X, ALU.add))
                then(nc.vector.scalar_tensor_tensor(small[:, :], small[:, :], 1e-6, chosen[:, :], ALU.mult, ALU.add))
                then(nc.vector.reciprocal(small[:, :], small[:, :]))
                then(nc.vector.tensor_tensor(gate[:, :, :], gate[:, :, :], per_token, ALU.mult))

            def take(n):
                name, c = JOBS[n]
                if name not in NO_PRODUCT:
                    dve.wait_ge(job_full, PRODUCTS[n])
                tiles = slice(c * TC, (c + 1) * TC)
                product = bank(n)
                by_tile = product.rearrange("p (t d) -> p t d", t=TC)
                if name == "L":
                    if c != 1:
                        dve.wait_ge(x_in[c], 16)
                        moments(c)
                    layernorm(c)
                elif name in ("T", "A", "X"):
                    then(nc.vector.tensor_copy(xnT[:, :], product))
                elif name in ("K", "KS", "Q", "QS"):
                    which = 0 if name[0] == "K" else 1
                    rotate(which, c, product, len(name) == 2)
                elif name == "KP":
                    split(0, c)
                elif name == "QP":
                    split(1, c)
                    bound(c)
                elif name == "V":
                    nc.vector.tensor_copy(va[:, tiles, :, 0:DH],
                                          product.rearrange("p (t h d) -> p t h d", t=TC, h=H)).then_inc(v_ready, 1)
                    dve.wait_ge(v_ready, c + 1)
                elif name[0] == "S":
                    if name == "S0":
                        wait_for_keys(dve, c)
                    pairs = slice(0, GH // 2) if name == "S0" else slice(GH // 2, NP)
                    for e in range(2):
                        ins = nc.vector.tensor_scalar(kst[0:ROWS, 2 * pairs.start + e:2 * pairs.stop:2, c * CH:(c + 1) * CH],
                                                      kpair[0:ROWS, pairs, :], own[0:ROWS, e:e + 1], None, ALU.mult)
                    ins.then_inc(keys_ready, 1)
                elif name == "B":
                    then(nc.vector.tensor_reduce(bmax[:, :], product[0:1, 0:H], AX.X, ALU.max))
                    nc.vector.tensor_scalar(flag[0:1, c:c + 1], bmax[:, :], BOUND / SCALE, None,
                                            ALU.is_gt).then_inc(flag_ready, 1)
                elif name[0] == "N":
                    g = int(name[1])
                    heads = product.rearrange("p (t j r) -> p t j r", t=TC, j=GH)
                    then(nc.vector.reciprocal(rec[:, :, :], heads[:, :, :, DH]))
                    then(nc.vector.tensor_tensor(
                        att[:, :, g * GH * DH:(g + 1) * GH * DH].rearrange("p t (j d) -> p t j d", j=GH),
                        heads[:, :, :, 0:DH], rec[:, :, :].unsqueeze(3).broadcast_to([P, TC, GH, DH]), ALU.mult))
                elif name == "O":
                    then(nc.vector.tensor_tensor(xs[:, tiles, :], by_tile, xs[:, tiles, :], ALU.add))
                elif name == "M":
                    moments(c, again=True)
                    layernorm(c, again=True)
                elif name == "R":
                    dve.wait_ge(ffn_in, 16 * 5)
                    then(nc.vector.tensor_tensor(lg[:, :, :], by_tile[:, :, RD:RD + E],
                                                 rbias[:, :].unsqueeze(1).broadcast_to([P, TC, E]), ALU.add))
                    then(nc.vector.tensor_reduce(small[:, :], lg[:, :, :], AX.X, ALU.max))
                    nc.vector.tensor_tensor(lg[:, :, :], lg[:, :, :], small[:, :].unsqueeze(2).broadcast_to([P, TC, E]),
                                            ALU.subtract).then_inc(logits_ready, 1)
                    then(nc.vector.tensor_copy(low_rank[:, :, 0:RD], by_tile[:, :, 0:RD]))
                elif name == "W":
                    dve.wait_ge(logits_exp, c + 1)
                    choose()
                    routed = low_rank[:, :, R:RD].rearrange("p t (e r) -> p t e r", e=E)
                    then(nc.vector.tensor_tensor(routed, routed,
                                                 gate[:, :, :].unsqueeze(3).broadcast_to([P, TC, E, R]), ALU.mult))
                elif name == "U":
                    then(nc.vector.tensor_copy(att[0:RD + 1, :, :].rearrange("p t d -> p (t d)"), product[0:RD + 1, :]))
                elif name == "F":
                    nc.vector.tensor_tensor(xs[:, tiles, :], by_tile, xs[:, tiles, :], ALU.add).then_inc(y_ready, 1)
                    dve.wait_ge(y_ready, c + 1)
                if n in FEEDS:
                    nc.vector.engine_nop().then_inc(job_fed, 1)

            def row_maxima(c):
                with dve.If(at_flag(dve, c) > 0):
                    dve.wait_ge(ident_in, 16)
                    dve.wait_ge(const_in, 16 * 4)
                    nc.vector.tensor_copy(idb[:, :], idf[:, :]).then_inc(max_masks[c], 1)
                    nc.vector.tensor_copy(futb[:, :], fut[:, :]).then_inc(max_masks[c], 1)
                    for t in range(TC):
                        width = (c * TC + t + 1) * P
                        with dve.Fori(0, NP) as pair:
                            for e in range(2):
                                dve.wait_ge(max_scores[c], t * H + pair * 2 + (e + 1))
                                nc.vector.tensor_reduce(
                                    rmax[:, t, bass.ds(pair * 2 + e, 1)],
                                    ps[:, :, :, :].rearrange("p a b q -> p (a b q)")[:, 0:width],
                                    AX.X, ALU.max).then_inc(max_taken[c], 1)
                    dve.wait_ge(max_taken[c], TC * H)
                    n = [0]

                    def after(ins):
                        n[0] += 1
                        ins.then_inc(max_vec[c], 1)
                        dve.wait_ge(max_vec[c], n[0])
                    after(nc.vector.tensor_scalar(mrest[:, :, :], rmax[:, :, :], -1.0, None, ALU.mult))
                    by_half = mbf[:, :, :].rearrange("p t (n e) -> p t e n", e=2)
                    for part in range(SHIFT_ROWS):
                        after(nc.vector.tensor_copy(mbf[:, :, :], mrest[:, :, :]))
                        for t in range(TC):
                            after(nc.vector.tensor_copy(mparts[:, t, :, part, :], by_half[:, t, :, :]))
                        if part + 1 < SHIFT_ROWS:
                            after(nc.vector.tensor_tensor(mrest[:, :, :], mrest[:, :, :], mbf[:, :, :], ALU.subtract))
                    dve.wait_ge(max_scores[c], TC * H + 1)
                    nc.vector.tensor_copy(mrow[:, :], ps[0:2 * SHIFT_ROWS * NP, 0, 0, :]).then_inc(max_rows[c], 1)
                    dve.wait_ge(max_rows[c], 1)
                nc.vector.engine_nop()

            nc.vector.memset(xnT[:, :], 0.0).then_inc(warm_ready, 1)
            nc.vector.memset(po[:, :], 0.0).then_inc(ones_set, 1)
            nc.vector.memset(kpair[SHIFT:ROWS, :, :].bitcast(F32), ONE_ONE).then_inc(ones_set, 1)
            nc.vector.memset(low_rank[:, :, RD:P], 1.0).then_inc(ones_set, 1)
            for n in range(FIRST_JOBS):
                take(n)
                if JOBS[n][0] == "T":
                    dve.wait_ge(x_in[1], 16)
                    moments(1)
            row_maxima(0)
            due = blocks_by_unit()
            for u in range(len(UNITS)):
                if u in FIRST_UNIT[1:]:
                    row_maxima(FIRST_UNIT.index(u))
                for b in due.get(u, ()):
                    if BLOCKS[b]["last"]:
                        evacuate(b)
                for n in JOBS_AT.get(u, ()):
                    take(n)
            evacuate(len(BLOCKS) - 1)
            for n in TAIL_JOBS:
                take(n)

        @block.tensor
        def _(pe):
            def scores(u):
                unit = UNITS[u]
                c, g, kt = unit["c"], unit["g"], unit["kt"]
                if u >= NS:
                    pe.wait_ge(exp_ready, u - NS + 1)
                per_pair = len(unit["pairs"])
                for at, pair in enumerate(unit["pairs"]):
                    for e in range(2):
                        head = g * GH + pair * 2 + e
                        for dk, q0, n, place in pieces(unit["kind"]):
                            bank = e if per_pair == 1 else at
                            place += 0 if per_pair == 1 else e * 2 * P
                            key = (kt + dk) * P
                            q = c * CH + q0
                            ins = nc.tensor.matmul(ps[:, u % NS, bank, place:place + n], kst[0:ROWS, head, key:key + P],
                                                   qst[0:ROWS, g * 2 + pair, q:q + n], start=True, stop=True)
                ins.then_inc(scores_ready, 1)

            def values(b):
                blk = BLOCKS[b]
                last_unit = blk["units"][-1]
                if blk["diagonal"]:
                    pe.wait_ge(masked, MASKS_THROUGH[last_unit])
                else:
                    pe.wait_ge(exp_ready, last_unit + 1)
                if blk["first"]:
                    pe.wait_ge(v_ready, blk["c"] + 1)
                    group = blk["c"] * NG + blk["g"]
                    if group:
                        pe.wait_ge(o_free, group)
                what = pieces(blk["kind"])
                for i, (dk, q0, n, place) in enumerate(what):
                    for j in range(GH):
                        head = blk["g"] * GH + j
                        if blk["kind"] == "mid":
                            buf, at = last_unit, j * 2 * P
                        else:
                            buf, at = blk["units"][j // 2], (j % 2) * CH + place
                        ins = nc.tensor.matmul(po[32 * j:32 * j + DH + 1, q0:q0 + n], va[:, blk["kt"] + dk, head, :],
                                               pbuf[:, buf % NPB, at:at + n], start=blk["first"],
                                               stop=blk["last"] and i + 1 == len(what), skip_group_check=True)
                ins.then_inc(block_done, 1)

            def base(product):
                for t in range(TC):
                    nc.tensor.matmul(product[:, t * P:(t + 1) * P], xnT[:, t * P:(t + 1) * P], wbase[:, :],
                                     start=t == 0, stop=False, skip_group_check=True)

            def job(n):
                name, c = JOBS[n]
                if name in NO_PRODUCT:
                    return
                pe.wait_ge(job_fed, fed(n))
                product = bank(n)
                tile = lambda t: slice(t * P, (t + 1) * P)
                if name in ("T", "A", "X"):
                    src = {"T": xn, "A": att, "X": xn}[name]
                    for t in range(TC):
                        ins = nc.tensor.transpose(product[:, tile(t)], src[:, t, :], idf[:, :])
                elif name in ("K", "KS", "Q", "QS"):
                    which = ("K", "KS", "Q", "QS").index(name)
                    ins = nc.tensor.matmul(product, wqkv[:, which, :], xnT[:, :], start=True, stop=True)
                elif name == "V":
                    for t in range(TC):
                        ins = nc.tensor.matmul(product[:, tile(t)], xnT[:, tile(t)], wqkv[:, 4, :], start=True, stop=True)
                elif name == "B":
                    pe.wait_ge(const_in, 16 * 4)
                    ins = nc.tensor.matmul(product[0:1, 0:H], bnd[:, :], hsum[:, :], start=True, stop=True)
                elif name[0] == "N":
                    g = int(name[1])
                    pe.wait_ge(o_free, c * NG + g + 1)
                    for t in range(TC):
                        ins = nc.tensor.transpose(product[:, tile(t)], oT[:, c % 2, g, tile(t)], idf[:, :])
                elif name == "O":
                    pe.wait_ge(ffn_in, 16 * 5)
                    for t in range(TC):
                        ins = nc.tensor.matmul(product[:, tile(t)], xnT[:, tile(t)], wout[:, :], start=True, stop=True)
                elif name == "R":
                    for t in range(TC):
                        ins = nc.tensor.matmul(product[:, t * P:t * P + RD + E], xnT[:, tile(t)], wdown[:, :],
                                               start=True, stop=True)
                    if n in TAIL_JOBS:
                        ins.then_inc(job_full, 1)
                        base(bank(TAIL_JOBS[-1]))
                        return
                elif name == "U":
                    for t in range(TC):
                        ins = nc.tensor.transpose(product[0:RD + 1, tile(t)], low_rank[:, t, 0:RD + 1], idf[:, :])
                elif name == "F":
                    if n not in TAIL_JOBS:
                        base(product)
                    for t in range(TC):
                        ins = nc.tensor.matmul(product[:, tile(t)], att[0:RD + 1, t, :], wup[:, :], start=False, stop=True,
                                               skip_group_check=True)
                ins.then_inc(job_full, 1)

            def row_maxima(c):
                with pe.If(at_flag(pe, c) > 0):
                    pe.wait_ge(max_masks[c], 2)
                    pe.wait_ge(keys_ready, 2 * c + 2)
                    wait_for_queries(pe, c)
                    if c:
                        pe.wait_ge(exp_ready, FIRST_UNIT[c])
                    for t in range(TC):
                        tile = c * TC + t
                        keys = (tile + 1) * P
                        with pe.Fori(0, NP) as pair:
                            for e in range(2):
                                if t == 0 and e == 0:
                                    with pe.If(pair > 0):
                                        pe.wait_ge(max_taken[c], pair * 2)
                                    pe.nop()
                                else:
                                    pe.wait_ge(max_taken[c], t * H + pair * 2 + e)
                                for k0 in range(0, keys, CH):
                                    n = min(CH, keys - k0)
                                    bank = k0 // CH
                                    edge = k0 + n == keys
                                    ins = nc.tensor.matmul(ps[:, bank // 2, bank % 2, 0:n],
                                                           qst[0:ROWS, bass.ds(pair, 1), tile * P:(tile + 1) * P],
                                                           kst[0:ROWS, bass.ds(pair * 2 + e, 1), k0:k0 + n],
                                                           start=True, stop=not edge, skip_group_check=True)
                                ins = nc.tensor.matmul(ps[:, bank // 2, bank % 2, n - P:n], idb[:, :], futb[:, :],
                                                       start=False, stop=True, skip_group_check=True)
                                ins.then_inc(max_scores[c], 1)
                    pe.wait_ge(max_taken[c], TC * H)
                    pe.wait_ge(max_vec[c], 1 + SHIFT_ROWS * (1 + TC) + SHIFT_ROWS - 1)
                    rows = 2 * SHIFT_ROWS * NP
                    for t in range(TC):
                        ins = nc.tensor.transpose(ps[0:rows, 0, 0, t * P:(t + 1) * P],
                                                  mparts[:, t, :, :, :].rearrange("p a b n -> p (a b n)"), idf[:, :])
                    ins.then_inc(max_scores[c], 1)
                    pe.wait_ge(max_stacked[c], 16)
                pe.nop()

            def keep_warm(times, left, right):
                for _ in range(times):
                    nc.tensor.matmul(ps[:, NS - 1, 1, :], left, right, start=True, stop=True)

            pe.wait_ge(warm_ready, 1)
            zeros = xnT[:, :].bitcast(BF16)
            keep_warm(WARM_START, zeros[:, 0:P], zeros[:, 0:CH])
            pe.wait_ge(ident_in, 16)
            pe.wait_ge(qkv_in, 16)
            for n in range(FIRST_JOBS):
                if JOBS[n][0] == "B":
                    keep_warm(WARM_PARTS, wqkv[:, 0, :], xnT[:, :])
                job(n)
            pe.wait_ge(ones_set, 3)
            pe.wait_ge(zeroed, 2)
            due = blocks_by_unit()
            for u in range(len(UNITS)):
                if u in FIRST_UNIT:
                    c = FIRST_UNIT.index(u)
                    row_maxima(c)
                    pe.wait_ge(keys_ready, 2 * c + 1)
                    wait_for_queries(pe, c)
                if u in SECOND_GROUP:
                    pe.wait_ge(keys_ready, 2 * SECOND_GROUP.index(u) + 2)
                scores(u)
                for b in due.get(u, ()):
                    values(b)
                for n in JOBS_AT.get(u, ()):
                    job(n)
            for u in range(len(UNITS), len(UNITS) + LAG):
                for b in due.get(u, ()):
                    values(b)
            for n in TAIL_JOBS:
                keep_warm(WARM.get(JOBS[n][0], 0), kst[0:ROWS, 0, 0:P], kst[0:ROWS, 0, 0:CH])
                job(n)


def rope_tables(order):
    inv = (np.float32(1.0) / np.float32(10000.0) ** (np.arange(0, DH, 2, dtype=np.float32) / np.float32(DH))).astype(np.float32)
    angle = (np.arange(S, dtype=np.float32)[:, None] * inv[None, :]).astype(np.float32)
    half = DH // 2
    d = order % DH
    cos, sin = np.cos(angle), np.sin(angle)
    sign = np.where(d < half, -1.0, 1.0).astype(np.float32)
    return np.ascontiguousarray(cos[:, d % half].T), np.ascontiguousarray((sin[:, d % half] * sign).T)


def kernel(L0_attn_x, L0_attn_w_qkv, L0_attn_w_out, L0_ffn_base_W, L0_ffn_base_b, L0_ffn_shared_A,
           L0_ffn_shared_B, L0_ffn_routed_A, L0_ffn_routed_B, L0_ffn_router_W, L0_ffn_router_b):
    from concourse import bacc
    from concourse.bass_utils import run_bass_kernel_spmd

    e, d, n = np.meshgrid(np.arange(2), np.arange(DH), np.arange(NP), indexing="ij")
    order = ((2 * n + e) * DH + d).reshape(-1)
    swapped = ((2 * n + e) * DH + (d + DH // 2) % DH).reshape(-1)
    w = np.asarray(L0_attn_w_qkv)
    w_q, w_k, w_v = w[:, :D], w[:, D:2 * D], w[:, 2 * D:]
    cos, sin = rope_tables(order)
    first = SWAPPED_PRODUCTS * CH
    sin[:, first:] = sin[np.arange(P) ^ HALF, first:]
    arrays = {
        "x": np.asarray(L0_attn_x).reshape(S, D),
        "w_qkv": np.stack([w_k[:, order], w_k[:, swapped], w_q[:, order], w_q[:, swapped], w_v], axis=1),
        "rope_c": cos,
        "rope_s": sin,
        "w_out": np.asarray(L0_attn_w_out),
        "w_down": np.concatenate([np.asarray(L0_ffn_shared_A), np.asarray(L0_ffn_routed_A).reshape(E * R, D),
                                  np.asarray(L0_ffn_router_W)]).T,
        "w_up": np.concatenate([np.asarray(L0_ffn_shared_B).T,
                                np.asarray(L0_ffn_routed_B).transpose(0, 2, 1).reshape(E * R, D),
                                np.asarray(L0_ffn_base_b)[None, :]]),
        "w_base": np.asarray(L0_ffn_base_W).T,
        "router_b": np.broadcast_to(np.asarray(L0_ffn_router_b)[None, :], (P, E)),
        "ident": np.eye(P, dtype=np.float32),
        "head_sum": (order[:, None] // DH == np.arange(H)[None, :]).astype(np.float32),
        "own_rows": (np.concatenate([np.arange(SHIFT) // DH % 2, np.arange(P - SHIFT) // SHIFT_ROWS])[:, None]
                     == np.arange(2)[None, :]).astype(np.float32),
        "lower": np.broadcast_to(np.tril(np.ones((E, E), np.float32), -1)[None], (P, E, E)),
        "future": np.triu(np.full((P, P), MASKED, np.float32), 1),
    }
    arrays = {name: np.ascontiguousarray(a) for name, a in arrays.items()}
    nc = bacc.Bacc("TRN2", target_bir_lowering=False, num_devices=1)
    args = {name: nc.dram_tensor(f"{name}_dram", a.shape, F32, kind="ExternalInput").ap() for name, a in arrays.items()}
    out = nc.dram_tensor("out_dram", (S, D), F32, kind="ExternalOutput").ap()
    build(nc, **args, out=out)
    result = run_bass_kernel_spmd(nc, [{f"{name}_dram": a for name, a in arrays.items()}], core_ids=[0])
    return result.results[0]["out_dram"].reshape(1, S, D)
```
